# Optimizing a Trainium2 kernel written in Bass

```python
import numpy as np
import jax
import jax.numpy as jnp

def _softmax(x, axis=-1):
    return jax.nn.softmax(x, axis=axis)

def _gelu(x):
    return jax.nn.gelu(x, approximate=True)

def _silu(x):
    return jax.nn.silu(x)

def _sigmoid(x):
    return jax.nn.sigmoid(x)

def _layernorm(x, axis=-1, eps=1e-05):
    m = jnp.mean(x, axis=axis, keepdims=True)
    v = jnp.var(x, axis=axis, keepdims=True)
    return (x - m) / jnp.sqrt(v + eps)

def _scatter_add(tgt, idx, src, axis=0):
    return tgt.at[idx].add(src)

def _segment_sum(src, seg, n):
    return jax.ops.segment_sum(src, seg, n)
kernel_name = 'mk_seq_preln_d1_jaxref_r4_d07f15'

def setup_inputs(seed: int=0):
    np.random.seed(seed)
    _w = jnp.asarray

    def _L0_attn_setup():
        import jax, jax.numpy as jnp
        import numpy as np
        D_MODEL = 256
        NUM_HEADS = 16
        D_HEAD = 64
        N_CTX = 512
        BATCH = 2
        SEQ = 512
        NEG = 10000000000.0
        key = jax.random.key(seed)
        kx, kk, kq, kv, ko = jax.random.split(key, 5)
        s = 1.0 / np.sqrt(D_MODEL)
        x = jax.random.normal(kx, (BATCH, SEQ, D_MODEL), dtype=jnp.float32)
        W_K = jax.random.normal(kk, (NUM_HEADS, D_HEAD, D_MODEL), dtype=jnp.float32) * s
        W_Q = jax.random.normal(kq, (NUM_HEADS, D_HEAD, D_MODEL), dtype=jnp.float32) * s
        W_V = jax.random.normal(kv, (NUM_HEADS, D_HEAD, D_MODEL), dtype=jnp.float32) * s
        W_O = jax.random.normal(ko, (D_MODEL, D_HEAD * NUM_HEADS), dtype=jnp.float32) * s
        return {'x': x, 'W_K': W_K, 'W_Q': W_Q, 'W_V': W_V, 'W_O': W_O}
    _L0_attn_in = _L0_attn_setup()

    def _L0_ffn_setup():
        import jax, jax.numpy as jnp
        import numpy as np
        NUM_EXPERTS = 8
        TOP_K = 2
        D_MODEL = 256
        EXPERT_CAP = 128
        B, S = (4, 512)
        key = jax.random.key(seed)
        ks = jax.random.split(key, 4)
        scale = 1.0 / np.sqrt(D_MODEL)
        x = jax.random.normal(ks[0], (B, S, D_MODEL), dtype=jnp.float32)
        gate_w = jax.random.normal(ks[1], (D_MODEL, NUM_EXPERTS), dtype=jnp.float32) * scale
        w1 = jax.random.normal(ks[2], (NUM_EXPERTS, D_MODEL, EXPERT_CAP), dtype=jnp.float32) * scale
        b1 = jnp.zeros((NUM_EXPERTS, EXPERT_CAP), dtype=jnp.float32)
        w2 = jax.random.normal(ks[3], (NUM_EXPERTS, EXPERT_CAP, D_MODEL), dtype=jnp.float32) * (1.0 / np.sqrt(EXPERT_CAP))
        b2 = jnp.zeros((NUM_EXPERTS, D_MODEL), dtype=jnp.float32)
        return {'x': x, 'gate_w': gate_w, 'w1': w1, 'b1': b1, 'w2': w2, 'b2': b2}
    _L0_ffn_in = _L0_ffn_setup()
    _d = {'L0_attn_x': _L0_attn_in['x'], 'L0_attn_W_K': _L0_attn_in['W_K'], 'L0_attn_W_Q': _L0_attn_in['W_Q'], 'L0_attn_W_V': _L0_attn_in['W_V'], 'L0_attn_W_O': _L0_attn_in['W_O'], 'L0_ffn_gate_w': _L0_ffn_in['gate_w'], 'L0_ffn_w1': _L0_ffn_in['w1'], 'L0_ffn_b1': _L0_ffn_in['b1'], 'L0_ffn_w2': _L0_ffn_in['w2'], 'L0_ffn_b2': _L0_ffn_in['b2']}
    _x0 = _d['L0_attn_x']
    _d['L0_attn_x'] = jax.random.normal(jax.random.fold_in(jax.random.key(seed), 1), (8, 512, 256), dtype=_x0.dtype)
    del _x0
    return _d

def reference(L0_attn_x, L0_attn_W_K, L0_attn_W_Q, L0_attn_W_V, L0_attn_W_O, L0_ffn_gate_w, L0_ffn_w1, L0_ffn_b1, L0_ffn_w2, L0_ffn_b2):

    def _L0_attn_ref(x, W_K, W_Q, W_V, W_O):
        import jax, jax.numpy as jnp
        import numpy as np
        D_MODEL = 256
        NUM_HEADS = 16
        D_HEAD = 64
        N_CTX = 512
        BATCH = 2
        SEQ = 512
        NEG = 10000000000.0
        B, S, D = x.shape
        k = jnp.einsum('ihd,bpd->biph', W_K, x)
        q = jnp.einsum('ihd,bpd->biph', W_Q, x)
        v = jnp.einsum('ihd,bpd->biph', W_V, x)
        scores = jnp.einsum('biph,biqh->biqp', k, q)
        mask = jnp.tril(jnp.ones((S, S), dtype=scores.dtype))
        masked = scores * mask - NEG * (1.0 - mask)
        attn = jax.nn.softmax(masked / np.sqrt(D_HEAD), axis=-1)
        z = jnp.einsum('biph,biqp->biqh', v, attn)
        z_flat = jnp.transpose(z, (0, 2, 1, 3)).reshape(B, S, -1)
        out = jnp.einsum('df,bqf->bqd', W_O, z_flat)
        return out

    def _L0_ffn_ref(x, gate_w, w1, b1, w2, b2):
        import jax, jax.numpy as jnp
        import numpy as np
        NUM_EXPERTS = 8
        TOP_K = 2
        D_MODEL = 256
        EXPERT_CAP = 128
        B, S = (4, 512)
        Bx, Sx, D = x.shape
        xt = x.reshape(-1, D)
        gates = jax.nn.softmax(xt @ gate_w, axis=-1)
        topk_g, topk_i = jax.lax.top_k(gates, TOP_K)
        tok_w = topk_g.sum(axis=-1)
        sel = (topk_i[:, :, None] == jnp.arange(NUM_EXPERTS)[None, None, :]).any(axis=1)
        h = jax.nn.gelu(jnp.einsum('nd,edh->enh', xt, w1) + b1[:, None, :], approximate=False)
        y = jnp.einsum('enh,ehd->end', h, w2) + b2[:, None, :]
        out = jnp.einsum('end,ne,n->nd', y, sel.astype(x.dtype), tok_w)
        return out.reshape(Bx, Sx, D)
    x = L0_attn_x
    x = x + _L0_attn_ref(_layernorm(x, axis=-1), L0_attn_W_K, L0_attn_W_Q, L0_attn_W_V, L0_attn_W_O)
    x = x + _L0_ffn_ref(_layernorm(x, axis=-1), L0_ffn_gate_w, L0_ffn_w1, L0_ffn_b1, L0_ffn_w2, L0_ffn_b2)
    return x

_drawn_inputs = setup_inputs


def setup_inputs(seed=0):
    import zlib

    import numpy as np

    out = dict(_drawn_inputs(seed))
    spreads = {'L0_ffn_b1': (0.0, 0.1), 'L0_ffn_b2': (0.0, 0.1)}
    factors = {}
    for name, (base, spread) in spreads.items():
        noise = np.random.default_rng([zlib.crc32(name.encode()), seed]).standard_normal(out[name].shape)
        drawn = base * np.exp(spread * noise) if base else spread * noise
        out[name] = jnp.asarray(drawn.astype(out[name].dtype))
    for name, factor in factors.items():
        out[name] = (out[name] * factor).astype(out[name].dtype)
    return out
```

```python
from contextlib import ExitStack

import concourse.bass as bass
from concourse import mybir

ALU = mybir.AluOpType
ACT = mybir.ActivationFunctionType
AX = mybir.AxisListType
F32 = mybir.dt.float32
F32R = mybir.dt.float32r

P = 128
BANK = 512
NEG = 10000000000.0
EPS = 1e-5
FLT_MAX = 3.4028234e38


def span(start, size):
    return bass.ds(start, size)


def wait(eng, sem, b, per_batch, k):
    if isinstance(b, int):
        if b * per_batch + k > 0:
            eng.wait_ge(sem, b * per_batch + k)
    else:
        eng.wait_ge(sem, b * per_batch + k)


def wait_alone(eng, sem, b, per_batch, k, passed):
    wait(eng, sem, b, per_batch, k)
    if not isinstance(b, int):
        eng.sem_inc(passed, 1)


def build_layer(nc, x, wq_t, wk_t, wv_t, wo_t, gate_w, w1, b1_t, w2, b2, out):
    NB, SEQ, D = x.shape
    F = wq_t.shape[1]
    NE, _, CAP = w1.shape
    DH = 64
    NH = F // DH
    NPAIR = NH // 2
    NT = SEQ // P
    NC = D // P
    NG = F // P
    HALF = NPAIR // 2
    SCALE = DH ** -0.5
    SW = P * NT * (NT + 1) // 2
    WSZ = NC * F
    assert SEQ == BANK and CAP == P and NC * F == NG * D == NE * NC * CAP == NE * D
    assert NT == 4 and NPAIR == 8 and NC == 2 and NB % 2 == 0 and NE == 8

    S_AT = [P * t * (t + 1) // 2 for t in range(NT)]
    PT_AT = {0: 0, 1: 512, 3: 896, 2: 1024}
    PT_UNITS = [((0,), 512), ((1, 3), 512), ((2,), 256)]
    SC_UNITS = [((3,), (0,)), ((2,), (0,)), ((1, 0), (0, 256))]

    AUX = 14
    K_V0LAST, K_O1, K_V1, K_XNT, K_O0, K_V0NEXT = 0, 1, 3, 7, 9, 11
    aux_o1_last = AUX * (NB - 1) + 3 + K_V0NEXT
    aux_moe = aux_o1_last + 2

    with ExitStack() as ctx:
        def sb(name, shape, dt=F32):
            return ctx.enter_context(nc.sbuf_tensor(name, shape, dt))

        def bank(name):
            return ctx.enter_context(nc.psum_tensor(name, [P, BANK], F32))

        def sem(name):
            return ctx.enter_context(nc.semaphore(name))

        x_sb = sb("x_sb", [P, NB * NT * D])
        w_split = sb("w_split", [P, 4 * 2 * WSZ], F32R)
        xnT = sb("xnT", [P, 2, 2, NC, SEQ], F32R)
        xn = sb("xn", [P, NT, D])
        k_dup = sb("k_dup", [P, 2, 2, 2, SEQ], F32R)
        q_stk = sb("q_stk", [P, 2, 2, SEQ], F32R)
        v_sb = sb("v_sb", [P, NT, F])
        s_sb = sb("s_sb", [P, 2, SW])
        pt_sb = sb("pt_sb", [P, 2, 2, SW])
        zT = sb("zT", [P, 2, HALF, SEQ], F32R)
        mask = sb("mask", [P, SEQ])
        ident = sb("ident", [P, P])
        bn_parts = sb("bn_parts", [P, NT, 6])
        bn_mv = sb("bn_mv", [P, NT, 2])
        var_eps = sb("var_eps", [P, NT])
        rstd = sb("rstd", [P, NT])
        minus_half = sb("minus_half", [P, NT])
        neg_max = sb("neg_max", [P, 2, NT])
        row_sum = sb("row_sum", [P, 2, NT])
        row_inv = sb("row_inv", [P, 2, NT])
        b1_sb = sb("b1_sb", [P, NE])
        gate_raw = sb("gate_raw", [P, NC, NE])
        before = sb("before", [P, NE, NE])
        logit = sb("logit", [P, NT, NE])
        lmax = sb("lmax", [P, NT])
        gate = sb("gate", [P, NT, NE])
        gsum = sb("gsum", [P, NT])
        sel_pad = sb("sel_pad", [P, NT, 32])
        tok_w = sb("tok_w", [P, 2, NT])
        selT = sb("selT", [P, P], F32R)
        sel_keep = sb("sel_keep", [P, 2, NT * NE])

        def w_part(i, part):
            return w_split[:, (2 * i + part) * WSZ:(2 * i + part + 1) * WSZ]

        wk, wq, wv = ([w_part(i, r).rearrange("p (c f) -> p c f", c=NC) for r in range(2)] for i in range(3))
        wo = [w_part(3, r).rearrange("p (g d) -> p g d", g=NG) for r in range(2)]

        w1s = [w_part(0, r).rearrange("p (e c h) -> p e c h", e=NE, c=NC) for r in range(2)]
        w2s = [w_part(1, r).rearrange("p (e d) -> p e d", e=NE) for r in range(2)]
        b2s = [w_part(2, 0)[:, r * NT * D:(r + 1) * NT * D].rearrange("p (t d) -> p t d", t=NT) for r in range(2)]
        gates_w = [w_part(2, 1)[:, r * NC * NE:(r + 1) * NC * NE].rearrange("p (c e) -> p c e", c=NC) for r in range(2)]
        w1_raw = v_sb[:, :, 0:SEQ]
        w2_raw = v_sb[:, :, SEQ:F]
        b2_raw = pt_sb[:, 0, 0, 0:NT * D].rearrange("p (t d) -> p t d", t=NT)
        h_sb = [s_sb[:, r, 0:SEQ] for r in range(2)]
        h_hi = [k_dup[:, 0, r, 0, :] for r in range(2)]
        h_lo = [k_dup[:, 0, r, 1, :] for r in range(2)]
        acc = [pt_sb[:, 1, r, 0:NT * D].rearrange("p (t d) -> p t d", t=NT) for r in range(2)]
        rank_a = pt_sb[:, 0, 1, 0:256].rearrange("p (t e f) -> p t e f", t=NT, e=NE)
        rank_b = pt_sb[:, 0, 1, 256:512].rearrange("p (t e f) -> p t e f", t=NT, e=NE)
        rank = pt_sb[:, 0, 1, 512:512 + NT * NE].rearrange("p (t e) -> p t e", t=NT)

        kq_bank = bank("kq_bank")
        aux_bank = bank("aux_bank")
        sc_bank = [bank(f"sc_bank{i}") for i in range(3)]
        pt_bank = [bank(f"pt_bank{i}") for i in range(2)]
        z_bank = bank("z_bank")
        up_bank = [kq_bank, pt_bank[0]]
        y_bank = [[sc_bank[0], sc_bank[1]], [sc_bank[2], pt_bank[1]]]
        route_bank = z_bank

        d_x0 = sem("d_x0")
        d_x = sem("d_x")
        d_w = [sem(f"d_attn_w{i}") for i in range(4)]
        d_small = sem("d_small")
        d_w1, d_w2, d_b2 = sem("d_w1"), sem("d_w2"), sem("d_b2")
        d_dup = sem("d_dup")
        d_out = sem("d_out")
        const_set = sem("const_set")
        w_hi, w_lo = sem("w_hi"), sem("w_lo")
        ln_step = sem("ln_step")
        rstd_ready = sem("rstd_ready")
        pool_step = sem("pool_step")
        xn_ready = sem("xn_ready")
        aux_ready, aux_free = sem("aux_ready"), sem("aux_free")
        xn_hi = sem("xn_hi")
        xn_lo = sem("xn_lo")
        kq_ready = sem("kq_ready")
        kq_hi, kq_lo = sem("kq_hi"), sem("kq_lo")
        v_ready = sem("v_ready")
        sc_ready = sem("sc_ready")
        sc_masked = sem("sc_masked")
        exp_done = sem("exp_done")
        inv_done = sem("inv_done")
        p_ready = sem("p_ready")
        pt_ready = sem("pt_ready")
        pt_copied = sem("pt_copied")
        z_ready = sem("z_ready")
        z_hi, z_lo = sem("z_hi"), sem("z_lo")
        up_ready = sem("up_ready")
        h_ready, h_hi_ready = sem("h_ready"), sem("h_hi_ready")
        h_lo_ready = sem("h_lo_ready")
        y_ready = sem("y_ready")
        y_added = sem("y_added")
        route_ready = sem("route_ready")
        route_free = sem("route_free")
        route_step = sem("route_step")
        route_exp = sem("route_exp")
        moe_w_hi, moe_w_lo = sem("moe_w_hi"), sem("moe_w_lo")
        res_ready = sem("res_ready")
        zero_sel = sem("zero_sel")
        passed = sem("passed")

        V1_SLOTS = [(2, 1), (3, 0), (3, 1), (4, 0)]
        XNT_SLOTS = [(4, 1), (5, 0)]
        O1_SLOTS = [(1, 1), (2, 0)]
        O0_SLOTS = [(5, 1), (6, 0)]
        V0_SLOTS = [(6, 1), (7, 0), (7, 1)]
        XNT_EXPERTS = [3, 4]
        LOGITS_AT, BIAS_AT = 5, 7
        ROUTE = 12
        ROUTE_HEAD = 2

        def wait_z_used(eng, b, p):
            if p < 0:
                wait(eng, aux_free, b, AUX, 3 + K_O0 + 2 - AUX)
            else:
                wait(eng, aux_free, b, AUX, 3 + (K_O1 if p < HALF else K_O0) + 2)

        block = ctx.enter_context(nc.Block())

        def batches(eng, body):
            with eng.Fori(1, NB - 2, 2) as i:
                body(i, 1)
                body(i + 1, 0)

        def x_tiles(b, t, n):
            return x_sb[:, span(b * (NT * D) + t * D, n * D)]

        w_raw = [pt_sb[:, i % 2, :, 0:WSZ // 2] for i in range(2)]

        @block.sync
        def _(sp):
            sp.dma_start(x_tiles(0, 0, NT).rearrange("p (t d) -> p t d", t=NT),
                         x[0].rearrange("(t p) d -> p t d", p=P)).then_inc(d_x0, 16)
            weights = [w.rearrange("(c p) f -> p c f", p=P) for w in (wk_t, wq_t, wv_t)]
            for i in range(3):
                if i >= 2:
                    sp.wait_ge(w_lo, i - 1)
                sp.dma_start(w_raw[i % 2], weights[i]).then_inc(d_w[i], 16)
            sp.wait_ge(w_lo, 2)
            for c in range(2):
                sp.dma_start(w_raw[1][:, c, :].rearrange("p (g d) -> p g d", g=NG // 2),
                             wo_t[c * (F // 2):(c + 1) * (F // 2), :].rearrange("(g p) d -> p g d", p=P))\
                  .then_inc(d_w[3], 16)
            for b in range(1, NB):
                sp.dma_start(x_tiles(b, 0, NT).rearrange("p (t d) -> p t d", t=NT),
                             x[b].rearrange("(t p) d -> p t d", p=P)).then_inc(d_x, 16)
            sp.dma_start(b1_sb[:, :], b1_t).then_inc(d_small, 16)
            sp.dma_start(gate_raw[:, :, :], gate_w.rearrange("(c p) e -> p c e", p=P)).then_inc(d_small, 16)

            def duplicate(b, per, k, buf):
                wait_alone(sp, kq_lo, b, 2 * per, 2 * k + 1, passed)
                wait(sp, d_dup, b, 32 * per, 32 * k)
                for head, (src, dst) in enumerate(((0, 64), (64, 0))):
                    sp.dma_start(k_dup[dst:dst + 64, buf, head, :, :].bitcast(F32),
                                 k_dup[src:src + 64, buf, head, :, :].bitcast(F32)).then_inc(d_dup, 16)

            def batch(b, last=False):
                for p in range(NPAIR):
                    if not (last and p == NPAIR - 1):
                        duplicate(b, NPAIR, p + 1, (p + 1) % 2)

            duplicate(0, 0, 0, 0)
            batch(0)
            batches(sp, lambda b, q: batch(b))
            batch(NB - 1, last=True)

            sp.wait_ge(z_ready, NPAIR * (NB - 1) + HALF)
            for a in range(NT):
                sp.dma_start(w1_raw[:, a, :].rearrange("p (e c h) -> p e c h", e=2, c=NC),
                             w1[2 * a:2 * a + 2].rearrange("e (c p) h -> p e c h", p=P)).then_inc(d_w1, 16)
            sp.wait_ge(z_ready, NPAIR * NB)
            for a in range(NT):
                sp.dma_start(w2_raw[:, a, :].rearrange("p (e d) -> p e d", e=2),
                             w2[2 * a:2 * a + 2].rearrange("e p d -> p e d")).then_inc(d_w2, 16)
            sp.wait_ge(zero_sel, 1)
            for t in range(NT):
                sp.dma_start(b2_raw[32 * t:32 * t + NE, t, :], b2).then_inc(d_b2, 16)

            with sp.Fori(0, NB) as m:
                sp.wait_ge(res_ready, m + 1)
                sp.dma_start(out[span(m, 1)].rearrange("b (t p) d -> p (b t) d", p=P),
                             x_tiles(m, 0, NT).rearrange("p (t d) -> p t d", t=NT)).then_inc(d_out, 16)
            sp.wait_ge(d_out, 16 * NB)

        @block.gpsimd
        def _(pool):
            pool.memset(minus_half[:, :], -0.5).then_inc(const_set, 1)
            pool.memset(ident[:, :], 0.0).then_inc(const_set, 1)
            pool.memset(mask[:, :], 0.0).then_inc(const_set, 1)
            pool.memset(before[:, :, :], 1.0).then_inc(const_set, 1)
            pool.memset(sel_pad[:, :, :], 0.0).then_inc(const_set, 1)
            pool.wait_ge(const_set, 5)
            pool.affine_select(out=ident[:, :], in_=ident[:, :], compare_op=ALU.not_equal, fill=1.0,
                               base=0, pattern=[[-1, P]], channel_multiplier=1).then_inc(const_set, 1)
            pool.affine_select(out=mask[:, SEQ - P:SEQ], in_=mask[:, SEQ - P:SEQ], compare_op=ALU.is_ge,
                               fill=-NEG, base=0, pattern=[[-1, P]], channel_multiplier=1).then_inc(const_set, 1)
            pool.affine_select(out=before[:, :, :], in_=before[:, :, :], compare_op=ALU.is_ge, fill=0.0,
                               base=-1, pattern=[[1, NE], [-1, NE]], channel_multiplier=0).then_inc(const_set, 1)

            def rsqrt(c, k):
                wait_alone(pool, ln_step, c, 2, 2 * k + 2, passed)
                pool.tensor_scalar(var_eps[:, :], bn_mv[:, :, 1], EPS, None, ALU.add).then_inc(pool_step, 1)
                wait(pool, pool_step, c, 1, k + 1)
                pool.tensor_tensor(rstd[:, :], var_eps[:, :], minus_half[:, :], ALU.pow).then_inc(rstd_ready, 1)

            rsqrt(0, 0)
            rsqrt(0, 1)
            batches(pool, lambda b, q: rsqrt(b, 1))
            rsqrt(NB, 0)

            pool.wait_ge(pt_copied, 3 * NH * NB)
            pool.wait_ge(z_ready, NPAIR * NB)
            pool.memset(b2_raw, 0.0).then_inc(zero_sel, 1)

            def lo_part(m, e):
                wait(pool, h_hi_ready, m, NE, e + 1)
                wait(pool, y_ready, m, NE, e - 1)
                pool.tensor_tensor(h_lo[e % 2], h_sb[e % 2], h_hi[e % 2].bitcast(F32), ALU.subtract)\
                    .then_inc(h_lo_ready, 1)

            def experts(m, last=False):
                for e in range(NE):
                    lo_part(m, e)
                    if e == 1 and not last:
                        rsqrt(m, NB + 1)

            experts(0)
            batches(pool, lambda m, q: experts(m))
            experts(NB - 1, last=True)

        @block.scalar
        def _(act):
            def weight_hi(i, src, dst, landed, count, done):
                act.wait_ge(landed, count)
                act.activation(dst, src, ACT.Copy).then_inc(done, 1)

            def xnt_hi(c, k, u, aux, ka, buf):
                b, per = aux
                wait(act, aux_ready, b, per, ka + 1)
                act.activation(xnT[:, buf, 0, u, :], aux_bank[:, :], ACT.Copy).then_inc(xn_hi, 1)

            def v_unit(b, k, half, t):
                wait(act, aux_ready, b, AUX, 3 + k + 1)
                act.activation(v_sb[:, t, half * SEQ:(half + 1) * SEQ], aux_bank[:, :], ACT.Copy)\
                   .then_inc(aux_free, 1)

            def k_hi(b, p, buf):
                wait(act, kq_ready, b, 2 * NPAIR, 2 * p + 1)
                wait(act, d_dup, b, 32 * NPAIR, 32 * (p - 1))
                for head in range(2):
                    r = slice(64 * head, 64 * head + 64)
                    last = act.activation(k_dup[r, buf, head, 0, :], kq_bank[r, :], ACT.Copy)
                last.then_inc(kq_hi, 1)

            def q_hi(b, p, buf):
                wait(act, kq_ready, b, 2 * NPAIR, 2 * p + 2)
                for head in range(2):
                    r = slice(64 * head, 64 * head + 64)
                    last = act.activation(q_stk[r, buf, head, :], kq_bank[r, :], ACT.Copy)
                last.then_inc(kq_hi, 1)

            def exps(b, h, order):
                for t in order:
                    wait(act, sc_masked, b, 4 * NH, 4 * h + NT - t)
                    s = s_sb[:, h % 2, S_AT[t]:S_AT[t] + P * (t + 1)]
                    act.activation(s, s, ACT.Exp, bias=neg_max[:, h % 2, t:t + 1], scale=-1.0,
                                   accum_out=row_sum[:, h % 2, t:t + 1]).then_inc(exp_done, 1)

            def pt_copy(b, h, unit):
                n = 3 * h + unit
                wait(act, pt_ready, b, 3 * NH, n + 1)
                tiles, width = PT_UNITS[unit]
                at = PT_AT[tiles[0]]
                pair = h // 2
                if unit == 0:
                    wait(act, z_ready, b, NPAIR, pair - 1)
                act.activation(pt_sb[:, pair % 2, h % 2, at:at + width], pt_bank[n % 2][:, 0:width], ACT.Copy)\
                   .then_inc(pt_copied, 1)

            def z_part(b, p):
                wait(act, z_ready, b, NPAIR, p + 1)
                wait_z_used(act, b, p)
                act.activation(zT[:, 0, p % HALF, :], z_bank[:, :], ACT.Copy).then_inc(z_hi, 1)

            def batch(b, q, first=False, last=False):
                for p in range(NPAIR):
                    for ab in range(2):
                        h = 2 * p + ab
                        has_prev = not (first and h == 0)
                        nxt = not (last and p == NPAIR - 1)
                        exps(b, h, (3, 2))
                        if nxt:
                            (k_hi if ab == 0 else q_hi)(b, p + 1, (p + 1) % 2)
                        exps(b, h, (1, 0))
                        slot = (p, ab)
                        if slot == (0, 0) and not first:
                            v_unit(b, K_V0LAST, 0, NT - 1)
                        if slot in V1_SLOTS:
                            t = V1_SLOTS.index(slot)
                            v_unit(b, K_V1 + t, 1, t)
                        if slot in XNT_SLOTS:
                            u = XNT_SLOTS.index(slot)
                            xnt_hi(b, 1, u, (b, AUX), 3 + K_XNT + u, 1 - q)
                        if slot in V0_SLOTS and not last:
                            t = V0_SLOTS.index(slot)
                            v_unit(b, K_V0NEXT + t, 0, t)
                        if ab == 0 and not (first and p < 2):
                            z_part(b, p - 2)
                        if has_prev:
                            for unit in range(3):
                                pt_copy(b, h - 1, unit)
                        if last and slot == (NPAIR - 1, 0):
                            weight_hi(0, w1_raw, w_part(0, 0).rearrange("p (a n) -> p a n", a=NT), d_w1, 16 * NT, moe_w_hi)

            for i in range(2):
                weight_hi(i, w_raw[i % 2], w_part(i, 0).rearrange("p (c f) -> p c f", c=2), d_w[i], 16, w_hi)
            for u in range(NC):
                xnt_hi(0, 0, u, (0, 0), u, 0)
            weight_hi(2, w_raw[0], w_part(2, 0).rearrange("p (c f) -> p c f", c=2), d_w[2], 16, w_hi)
            k_hi(0, 0, 0)
            q_hi(0, 0, 0)
            weight_hi(3, w_raw[1], w_part(3, 0).rearrange("p (c f) -> p c f", c=2), d_w[3], 32, w_hi)
            for t in range(NT):
                v_unit(0, 2 + t - 3, 0, t)
            batch(0, 0, first=True)
            batches(act, lambda b, q: batch(b, q))
            batch(NB - 1, 1, last=True)
            z_part(NB, -2)
            for unit in range(3):
                pt_copy(NB, -1, unit)
            z_part(NB, -1)

            act.wait_ge(aux_free, aux_moe)
            weight_hi(2, gate_raw[:, :, :], gates_w[0], d_small, 32, moe_w_hi)
            weight_hi(1, w2_raw, w_part(1, 0).rearrange("p (a n) -> p a n", a=NT), d_w2, 16 * NT, moe_w_hi)
            weight_hi(2, b2_raw, b2s[0], d_b2, 16 * NT, moe_w_hi)

            def route_exp_part(m, k):
                wait(act, route_step, m, ROUTE, ROUTE * k + ROUTE_HEAD)
                act.activation(gate[:, :, :], logit[:, :, :], ACT.Exp).then_inc(route_exp, 1)

            def bias_part(m, k, q):
                wait(act, route_ready, m, 4, 4 * k + 2)
                act.activation(selT[:, :], route_bank[:, 0:P], ACT.Copy).then_inc(route_free, 1)
                for u in range(2):
                    wait(act, route_ready, m, 4, 4 * k + 3 + u)
                    wait(act, res_ready, m, 1, k - 1)
                    act.activation(acc[q][:, 2 * u:2 * u + 2, :],
                                   route_bank[:, :].rearrange("p (t d) -> p t d", t=2), ACT.Copy)\
                       .then_inc(route_free, 1)

            def gelu(m, e):
                wait(act, up_ready, m, NE, e + 1)
                wait(act, h_lo_ready, m, NE, e - 1)
                act.activation(h_sb[e % 2], up_bank[e % 2][:, :], ACT.Gelu, bias=b1_sb[:, e:e + 1])\
                   .then_inc(h_ready, 1)
                wait(act, h_ready, m, NE, e + 1)
                wait(act, y_ready, m, NE, e - 1)
                act.activation(h_hi[e % 2], h_sb[e % 2], ACT.Copy).then_inc(h_hi_ready, 1)

            def experts(m, q, last=False):
                for e in range(NE):
                    gelu(m, e)
                    if not last and e in XNT_EXPERTS:
                        u = XNT_EXPERTS.index(e)
                        xnt_hi(m, NB + 1, u, (m, 2), aux_moe + u, 1 - q)
                    if not last and e == LOGITS_AT:
                        route_exp_part(m, 1)
                    if not last and e == BIAS_AT:
                        bias_part(m, 1, 1 - q)

            route_exp_part(0, 0)
            bias_part(0, 0, 0)
            experts(0, 0)
            batches(act, lambda m, q: experts(m, q))
            experts(NB - 1, 1, last=True)

        @block.vector
        def _(dve):
            def weight_lo(src, hi, dst, ready, count, done):
                dve.wait_ge(ready, count)
                dve.tensor_tensor(dst, src, hi.bitcast(F32), ALU.subtract).then_inc(done, 1)

            def stats(c, k, b):
                for t in range(NT):
                    last = dve.bn_stats(bn_parts[:, t, :], x_tiles(b, t, 1))
                last.then_inc(ln_step, 1)
                wait_alone(dve, ln_step, c, 2, 2 * k + 1, passed)
                for t in range(NT):
                    last = dve.bn_aggr(bn_mv[:, t, :], bn_parts[:, t, :])
                last.then_inc(ln_step, 1)

            def normalise(c, k, b, aux, ka):
                wait(dve, rstd_ready, c, 1, k + 1)
                wait(dve, aux_ready, *aux, ka)
                for t in range(NT):
                    last = dve.tensor_scalar(xn[:, t, :], x_tiles(b, t, 1), bn_mv[:, t, 0:1],
                                             rstd[:, t:t + 1], ALU.subtract, ALU.mult)
                last.then_inc(xn_ready, 1)

            def xnt_lo(c, k, u, buf):
                wait(dve, xn_hi, c, 2, 2 * k + u + 1)
                dve.tensor_tensor(xnT[:, buf, 1, u, :], aux_bank[:, :], xnT[:, buf, 0, u, :].bitcast(F32),
                                  ALU.subtract).then_inc(aux_free, 1)

            def k_lo(b, p, buf):
                wait(dve, kq_hi, b, 2 * NPAIR, 2 * p + 1)
                for head in range(2):
                    r = slice(64 * head, 64 * head + 64)
                    last = dve.tensor_tensor(k_dup[r, buf, head, 1, :], kq_bank[r, :],
                                             k_dup[r, buf, head, 0, :].bitcast(F32), ALU.subtract)
                last.then_inc(kq_lo, 1)

            def q_lo(b, p, buf):
                wait(dve, kq_hi, b, 2 * NPAIR, 2 * p + 2)
                for head in range(2):
                    r = slice(64 * head, 64 * head + 64)
                    o = slice(64 - 64 * head, 128 - 64 * head)
                    last = dve.tensor_tensor(q_stk[o, buf, head, :], kq_bank[r, :],
                                             q_stk[r, buf, head, :].bitcast(F32), ALU.subtract)
                last.then_inc(kq_lo, 1)

            def mask_and_max(b, h):
                wait(dve, pt_ready, b, 3 * NH, 3 * (h - 1))
                for unit, (tiles, cols) in enumerate(SC_UNITS):
                    wait_alone(dve, sc_ready, b, 3 * NH, 3 * h + unit + 1, passed)
                    for t, at in zip(tiles, cols):
                        n = P * (t + 1)
                        dve.tensor_tensor_reduce(
                            out=s_sb[:, h % 2, S_AT[t]:S_AT[t] + n], in0=sc_bank[unit][:, at:at + n],
                            in1=mask[:, SEQ - n:SEQ], scale=-SCALE, scalar=FLT_MAX, op0=ALU.add, op1=ALU.min,
                            accum_out=neg_max[:, h % 2, t:t + 1]).then_inc(sc_masked, 1)

            def divide(b, h):
                for i, (lo_t, hi_t) in enumerate(((2, 4), (0, 2))):
                    wait(dve, exp_done, b, 4 * NH, 4 * h + 2 * i + 2)
                    dve.reciprocal(row_inv[:, h % 2, lo_t:hi_t], row_sum[:, h % 2, lo_t:hi_t]).then_inc(inv_done, 1)
                    wait(dve, inv_done, b, 2 * NH, 2 * h + i + 1)
                    for t in (hi_t - 1, lo_t):
                        s = s_sb[:, h % 2, S_AT[t]:S_AT[t] + P * (t + 1)]
                        last = dve.tensor_scalar(s, s, row_inv[:, h % 2, t:t + 1], None, ALU.mult)
                    last.then_inc(p_ready, 1)

            def z_part(b, p):
                wait(dve, z_hi, b, NPAIR, p + 1)
                dve.tensor_tensor(zT[:, 1, p % HALF, :], z_bank[:, :], zT[:, 0, p % HALF, :].bitcast(F32),
                                  ALU.subtract).then_inc(z_lo, 1)

            def add_output(b, k, b_x, u):
                wait(dve, aux_ready, b, AUX, 3 + k + 1)
                dve.tensor_tensor(x_tiles(b_x, 2 * u, 2), x_tiles(b_x, 2 * u, 2), aux_bank[:, :], ALU.add)\
                   .then_inc(aux_free, 1)

            def batch(b, q, first=False, last=False):
                for p in range(NPAIR):
                    for ab in range(2):
                        h = 2 * p + ab
                        nxt = not (last and p == NPAIR - 1)
                        slot = (p, ab)
                        mask_and_max(b, h)
                        if nxt:
                            (k_lo if ab == 0 else q_lo)(b, p + 1, (p + 1) % 2)
                        divide(b, h)
                        if slot in O1_SLOTS and not first:
                            u = O1_SLOTS.index(slot)
                            add_output(b, K_O1 + u, b - 1, u)
                        if slot in O0_SLOTS:
                            u = O0_SLOTS.index(slot)
                            add_output(b, K_O0 + u, b, u)
                        if slot in XNT_SLOTS:
                            xnt_lo(b, 1, XNT_SLOTS.index(slot), 1 - q)
                        if ab == 0 and not (first and p < 2):
                            z_part(b, p - 2)
                        b_next = 0 if last else b + 1
                        if slot == (2, 0):
                            if first:
                                dve.wait_ge(d_x, 16 * (NB - 1))
                            stats(b, 1, b_next)
                        if slot == (3, 0):
                            normalise(b, 1, b_next, (b, AUX), 3 + K_XNT - AUX + 2)
                        if last and slot == (NPAIR - 1, 0):
                            weight_lo(w1_raw, w_part(0, 0).rearrange("p (a n) -> p a n", a=NT),
                                      w_part(0, 1).rearrange("p (a n) -> p a n", a=NT), moe_w_hi, 1, moe_w_lo)

            dve.wait_ge(d_x0, 16)
            stats(0, 0, 0)
            normalise(0, 0, 0, (0, 0), 0)
            for i in range(2):
                weight_lo(w_raw[i], w_part(i, 0).rearrange("p (c f) -> p c f", c=2),
                          w_part(i, 1).rearrange("p (c f) -> p c f", c=2), w_hi, i + 1, w_lo)
            for u in range(NC):
                xnt_lo(0, 0, u, 0)
            weight_lo(w_raw[0], w_part(2, 0).rearrange("p (c f) -> p c f", c=2),
                      w_part(2, 1).rearrange("p (c f) -> p c f", c=2), w_hi, 3, w_lo)
            k_lo(0, 0, 0)
            q_lo(0, 0, 0)
            weight_lo(w_raw[1], w_part(3, 0).rearrange("p (c f) -> p c f", c=2),
                      w_part(3, 1).rearrange("p (c f) -> p c f", c=2), w_hi, 4, w_lo)
            dve.wait_ge(const_set, 8)
            batch(0, 0, first=True)
            batches(dve, lambda b, q: batch(b, q))
            batch(NB - 1, 1, last=True)
            z_part(NB, -2)
            z_part(NB, -1)
            for u in range(2):
                dve.wait_ge(aux_ready, aux_o1_last + u + 1)
                dve.tensor_tensor(x_tiles(NB - 1, 2 * u, 2), x_tiles(NB - 1, 2 * u, 2), aux_bank[:, :], ALU.add)\
                   .then_inc(aux_free, 1)

            weight_lo(gate_raw[:, :, :], gates_w[0], gates_w[1], moe_w_hi, 2, moe_w_lo)
            weight_lo(w2_raw, w_part(1, 0).rearrange("p (a n) -> p a n", a=NT),
                      w_part(1, 1).rearrange("p (a n) -> p a n", a=NT), moe_w_hi, 3, moe_w_lo)
            weight_lo(b2_raw, b2s[0], b2s[1], moe_w_hi, 4, moe_w_lo)

            def linker(m, k, first):
                step = [first]

                def link(ins):
                    step[0] += 1
                    ins.then_inc(route_step, 1)
                    wait(dve, route_step, m, ROUTE, ROUTE * k + step[0])

                return link, step

            def route_head(m, k):
                link, step = linker(m, k, 0)
                lg = route_bank[:, 0:NT * NE].rearrange("p (t e) -> p t e", t=NT)
                tile_bc = [P, NT, NE]
                wait(dve, route_ready, m, 4, 4 * k + 1)
                link(dve.tensor_reduce(lmax[:, :], lg, AX.X, ALU.max))
                ins = dve.tensor_tensor(logit[:, :, :], lg, lmax[:, :].unsqueeze(2).broadcast_to(tile_bc), ALU.subtract)
                link(ins)
                assert step[0] == ROUTE_HEAD

            def route_tail(m, k, q):
                link, step = linker(m, k, ROUTE_HEAD)
                tile_bc = [P, NT, NE]
                wait(dve, route_exp, m, 1, k + 1)
                link(dve.tensor_reduce(gsum[:, :], gate[:, :, :], AX.X, ALU.add))
                link(dve.reciprocal(gsum[:, :], gsum[:, :]))
                link(dve.tensor_tensor(gate[:, :, :], gate[:, :, :], gsum[:, :].unsqueeze(2).broadcast_to(tile_bc), ALU.mult))
                other = gate[:, :, :].unsqueeze(2).broadcast_to([P, NT, NE, NE])
                own = gate[:, :, :].unsqueeze(3).broadcast_to([P, NT, NE, NE])
                dve.tensor_tensor(rank_a, other, own, ALU.is_gt)
                link(dve.tensor_tensor(rank_b, other, own, ALU.is_equal))
                link(dve.tensor_tensor(rank_b, rank_b, before[:, :, :].unsqueeze(1).broadcast_to([P, NT, NE, NE]),
                                       ALU.mult))
                link(dve.tensor_tensor(rank_a, rank_a, rank_b, ALU.add))
                link(dve.tensor_reduce(rank, rank_a, AX.X, ALU.add))
                wait(dve, route_ready, m, 4, 4 * k - 2)
                dve.tensor_scalar(sel_keep[:, q, :].rearrange("p (t e) -> p t e", t=NT), rank, 1.5, None, ALU.is_lt)
                link(dve.tensor_scalar(sel_pad[:, :, 0:NE], rank, 1.5, None, ALU.is_lt))
                link(dve.tensor_tensor(gate[:, :, :], gate[:, :, :], sel_pad[:, :, 0:NE], ALU.mult))
                link(dve.tensor_reduce(tok_w[:, q, :], gate[:, :, :], AX.X, ALU.add))
                assert step[0] == ROUTE

            def sum_expert(m, e, q):
                if e == 0:
                    wait(dve, route_free, m, 3, 3)
                for u in range(2):
                    if u == 0:
                        wait(dve, y_ready, m, NE, e + 1)
                    wait(dve, y_added, m, 2 * NE, 2 * e + u - 1)
                    for t in (2 * u, 2 * u + 1):
                        last = dve.scalar_tensor_tensor(
                            acc[q][:, t, :], y_bank[e % 2][u][:, (t % 2) * D:(t % 2) * D + D],
                            sel_keep[:, q, t * NE + e:t * NE + e + 1], acc[q][:, t, :], ALU.mult, ALU.add)
                    last.then_inc(y_added, 1)

            def result(m, q):
                wait(dve, y_added, m, 2 * NE, 2 * NE)
                for t in range(NT):
                    last = dve.scalar_tensor_tensor(x_tiles(m, t, 1), acc[q][:, t, :], tok_w[:, q, t:t + 1],
                                                    x_tiles(m, t, 1), ALU.mult, ALU.add)
                last.then_inc(res_ready, 1)

            def experts(m, q, last=False):
                for e in range(NE):
                    if not last and e == 0:
                        stats(m, NB + 1, m + 1)
                    sum_expert(m, e, q)
                    if not last and e == 1:
                        normalise(m, NB + 1, m + 1, (m, 2), aux_moe)
                    if not last and e + 1 in XNT_EXPERTS:
                        xnt_lo(m, NB + 1, XNT_EXPERTS.index(e + 1), 1 - q)
                    if not last and e + 1 == LOGITS_AT:
                        route_head(m, 1)
                    if not last and e == LOGITS_AT:
                        route_tail(m, 1, 1 - q)
                result(m, q)

            route_head(0, 0)
            route_tail(0, 0, 0)
            experts(0, 0)
            batches(dve, lambda m, q: experts(m, q))
            experts(NB - 1, 1, last=True)

        @block.tensor
        def _(pe):
            def split_product(out_ap, pairs):
                terms = [(s[i], v[j]) for s, v in pairs for i, j in ((0, 0), (0, 1), (1, 0))]
                for n, (s, v) in enumerate(terms):
                    last = pe.matmul(out_ap, s, v, start=(n == 0), stop=(n == len(terms) - 1))
                return last

            def k_or_q(b, p, w, unit, buf, cols):
                wait(pe, kq_lo, b, 2 * NPAIR, 2 * p + unit)
                split_product(kq_bank[:, :],
                              [([w[r][:, c, cols * P:(cols + 1) * P] for r in range(2)],
                                [xnT[:, buf, r, c, :] for r in range(2)]) for c in range(NC)]).then_inc(kq_ready, 1)

            def v_unit(b, k, half, t, buf):
                wait_aux(b, k)
                split_product(aux_bank[:, :],
                              [([xnT[:, buf, r, c, t * P:(t + 1) * P] for r in range(2)],
                                [wv[r][:, c, half * SEQ:(half + 1) * SEQ] for r in range(2)]) for c in range(NC)])\
                    .then_inc(aux_ready, 1)

            def wait_aux(b, k):
                wait(pe, aux_free, b, AUX, 3 + k)

            def xnt_unit(u):
                for t in range(NT):
                    last = pe.transpose(aux_bank[:, t * P:(t + 1) * P], xn[:, t, u * P:(u + 1) * P], ident[:, :])
                last.then_inc(aux_ready, 1)

            def output_unit(u, half):
                for t in (2 * u, 2 * u + 1):
                    last = split_product(aux_bank[:, (t % 2) * D:(t % 2) * D + D],
                                         [([zT[:, r, g, t * P:(t + 1) * P] for r in range(2)],
                                           [wo[r][:, half * HALF + g, :] for r in range(2)]) for g in range(HALF)])
                last.then_inc(aux_ready, 1)

            def scores(b, h):
                p, head = h // 2, h % 2
                if head == 0:
                    wait(pe, kq_lo, b, 2 * NPAIR, 2 * p + 2)
                    wait(pe, d_dup, b, 32 * NPAIR, 32 * (p + 1))
                for unit, (tiles, cols) in enumerate(SC_UNITS):
                    wait(pe, sc_masked, b, 4 * NH, 4 * (h - 1) + (1, 2, 4)[unit])
                    for t, at in zip(tiles, cols):
                        n = P * (t + 1)
                        for part in range(2):
                            last = pe.matmul(sc_bank[unit][:, at:at + n],
                                             q_stk[:, p % 2, head, t * P:(t + 1) * P],
                                             k_dup[:, p % 2, head, part, 0:n], start=(part == 0), stop=(part == 1))
                    last.then_inc(sc_ready, 1)

            def transposes(b, h):
                wait(pe, p_ready, b, 2 * NH, 2 * (h + 1))
                for unit, (keys, _) in enumerate(PT_UNITS):
                    n = 3 * h + unit
                    wait(pe, pt_copied, b, 3 * NH, n - 1)
                    at = 0
                    for j in keys:
                        for t in range(j, NT):
                            col = S_AT[t] + j * P
                            last = pe.transpose(pt_bank[n % 2][:, at:at + P], s_sb[:, h % 2, col:col + P], ident[:, :])
                            at += P
                    last.then_inc(pt_ready, 1)

            def head_outputs(b, p):
                wait(pe, pt_copied, b, 3 * NH, 6 * (p + 1))
                wait(pe, z_lo, b, NPAIR, p)
                if p == 0:
                    wait_aux(b, K_V1 if isinstance(b, int) and b == 0 else K_V0LAST + 1)
                if p == HALF:
                    wait_aux(b, K_V1 + NT)
                for j in range(NT):
                    for head in range(2):
                        n = SEQ - j * P
                        f = (2 * p + head) % NH * DH
                        last = pe.matmul(z_bank[64 * head:64 * head + 64, j * P:SEQ], v_sb[:, j, f:f + DH],
                                         pt_sb[:, p % 2, head, PT_AT[j]:PT_AT[j] + n],
                                         start=(j == 0), stop=(j == NT - 1))
                last.then_inc(z_ready, 1)

            def batch(b, q, first=False, last=False):
                for p in range(NPAIR):
                    for ab in range(2):
                        h = 2 * p + ab
                        slot = (p, ab)
                        scores(b, h)
                        if not (last and p == NPAIR - 1):
                            buf = q if p < NPAIR - 1 else 1 - q
                            k_or_q(b, p + 1, (wk, wq)[ab], ab, buf, (p + 1) % NPAIR)
                        if slot == (0, 0) and not first:
                            v_unit(b, K_V0LAST, 0, NT - 1, q)
                        if slot in O1_SLOTS and not first:
                            u = O1_SLOTS.index(slot)
                            wait(pe, z_lo, b, NPAIR, 0)
                            wait_aux(b, K_O1 + u)
                            output_unit(u, 1)
                        if slot in V1_SLOTS:
                            t = V1_SLOTS.index(slot)
                            v_unit(b, K_V1 + t, 1, t, q)
                        if slot in XNT_SLOTS:
                            u = XNT_SLOTS.index(slot)
                            wait(pe, xn_ready, b, 1, 2)
                            wait_aux(b, K_XNT + u)
                            xnt_unit(u)
                        if slot in O0_SLOTS:
                            u = O0_SLOTS.index(slot)
                            wait(pe, z_lo, b, NPAIR, HALF)
                            wait_aux(b, K_O0 + u)
                            output_unit(u, 0)
                        if slot in V0_SLOTS and not last:
                            t = V0_SLOTS.index(slot)
                            v_unit(b, K_V0NEXT + t, 0, t, 1 - q)
                        if not (first and h == 0):
                            transposes(b, h - 1)
                        if ab == 1 and not (first and p == 0):
                            head_outputs(b, p - 1)

            pe.wait_ge(const_set, 6)
            pe.wait_ge(xn_ready, 1)
            for u in range(NC):
                wait(pe, aux_free, 0, 0, u)
                xnt_unit(u)
            pe.wait_ge(aux_free, NC)
            pe.wait_ge(w_lo, 1)
            k_or_q(0, 0, wk, 0, 0, 0)
            pe.wait_ge(w_lo, 2)
            k_or_q(0, 0, wq, 1, 0, 0)
            pe.wait_ge(w_lo, 3)
            for t in range(NT):
                v_unit(0, 2 + t - 3, 0, t, 0)
            pe.wait_ge(w_lo, 4)
            batch(0, 0, first=True)
            batches(pe, lambda b, q: batch(b, q))
            batch(NB - 1, 1, last=True)
            transposes(NB, -1)
            head_outputs(NB, -1)
            for u in range(2):
                pe.wait_ge(z_lo, NPAIR * NB)
                pe.wait_ge(aux_free, aux_o1_last + u)
                output_unit(u, 1)

            def logits_unit(m, k, buf):
                wait(pe, route_free, m, 3, 3 * k)
                wait(pe, aux_free, m, 2, aux_moe + 2 * (k - 1) + 2)
                for t in range(NT):
                    last = split_product(route_bank[:, t * NE:(t + 1) * NE],
                                         [([xnT[:, buf, r, c, t * P:(t + 1) * P] for r in range(2)],
                                           [gates_w[r][:, c, :] for r in range(2)]) for c in range(NC)])
                last.then_inc(route_ready, 1)

            def bias_units(m, k):
                wait(pe, route_step, m, ROUTE, ROUTE * k + 10)
                pe.transpose(route_bank[:, 0:P], sel_pad[:, :, :].rearrange("p t e -> p (t e)"), ident[:, :])\
                  .then_inc(route_ready, 1)
                for u in range(2):
                    wait(pe, route_free, m, 3, 3 * k + 1 + u)
                    for t in (2 * u, 2 * u + 1):
                        for r in range(2):
                            last = pe.matmul(route_bank[:, (t % 2) * D:(t % 2) * D + D], selT[:, :], b2s[r][:, t, :],
                                             start=(r == 0), stop=(r == 1))
                    last.then_inc(route_ready, 1)

            def up(m, e, q):
                wait(pe, h_ready, m, NE, e - 1)
                split_product(up_bank[e % 2][:, :],
                              [([w1s[r][:, e, c, :] for r in range(2)],
                                [xnT[:, q, r, c, :] for r in range(2)]) for c in range(NC)]).then_inc(up_ready, 1)

            def down(m, e):
                wait(pe, h_lo_ready, m, NE, e + 1)
                for u in range(2):
                    wait(pe, y_added, m, 2 * NE, 2 * (e - 2) + u + 1)
                    for t in (2 * u, 2 * u + 1):
                        last = split_product(y_bank[e % 2][u][:, (t % 2) * D:(t % 2) * D + D],
                                             [([h_hi[e % 2][:, t * P:(t + 1) * P], h_lo[e % 2][:, t * P:(t + 1) * P]],
                                               [w2s[r][:, e % NE, :] for r in range(2)])])
                last.then_inc(y_ready, 1)

            def experts(m, q, first=False, last=False):
                for e in range(NE):
                    up(m, e, q)
                    if not last and e in XNT_EXPERTS:
                        u = XNT_EXPERTS.index(e)
                        wait(pe, xn_ready, m, 1, NB + 2)
                        wait(pe, aux_free, m, 2, aux_moe + u)
                        xnt_unit(u)
                    if not last and e == LOGITS_AT:
                        logits_unit(m, 1, 1 - q)
                    if not (first and e == 0):
                        down(m, e - 1)
                    if not last and e == BIAS_AT:
                        bias_units(m, 1)

            pe.wait_ge(aux_free, aux_moe)
            pe.wait_ge(moe_w_lo, 2)
            logits_unit(0, 0, 0)
            pe.wait_ge(moe_w_lo, 4)
            bias_units(0, 0)
            experts(0, 0, first=True)
            batches(pe, lambda m, q: experts(m, q))
            experts(NB - 1, 1, last=True)
            down(NB, -1)


def kernel(L0_attn_x, L0_attn_W_K, L0_attn_W_Q, L0_attn_W_V, L0_attn_W_O, L0_ffn_gate_w,
           L0_ffn_w1, L0_ffn_b1, L0_ffn_w2, L0_ffn_b2):
    import numpy as np
    import concourse.bacc as bacc
    from concourse.bass_utils import run_bass_kernel_spmd

    def rows(w):
        w = np.asarray(w)
        return np.ascontiguousarray(w.reshape(-1, w.shape[-1]).T)

    arrays = {
        "x": np.ascontiguousarray(L0_attn_x),
        "wq_t": rows(L0_attn_W_Q),
        "wk_t": rows(L0_attn_W_K),
        "wv_t": rows(L0_attn_W_V),
        "wo_t": np.ascontiguousarray(np.asarray(L0_attn_W_O).T),
        "gate_w": np.ascontiguousarray(L0_ffn_gate_w),
        "w1": np.ascontiguousarray(L0_ffn_w1),
        "b1_t": np.ascontiguousarray(np.asarray(L0_ffn_b1).T),
        "w2": np.ascontiguousarray(L0_ffn_w2),
        "b2": np.ascontiguousarray(L0_ffn_b2),
    }
    nc = bacc.Bacc("TRN2", target_bir_lowering=False, num_devices=1)
    args = {k: nc.dram_tensor(k, a.shape, mybir.dt.from_np(a.dtype), kind="ExternalInput").ap()
            for k, a in arrays.items()}
    y = nc.dram_tensor("y", arrays["x"].shape, F32, kind="ExternalOutput").ap()
    build_layer(nc, out=y, **args)
    r = run_bass_kernel_spmd(nc, [arrays], core_ids=[0])
    return r.results[0]["y"]
```

```python
from contextlib import ExitStack

import concourse.bass as bass
from concourse import mybir

ALU = mybir.AluOpType
ACT = mybir.ActivationFunctionType
AX = mybir.AxisListType
F32 = mybir.dt.float32
F32R = mybir.dt.float32r

P = 128
BANK = 512
NEG = 10000000000.0
EPS = 1e-5
EULER = 2.718281828459045
FLT_MAX = 3.4028234e38


def span(start, size):
    return bass.ds(start, size)


def wait(eng, sem, b, per_batch, k):
    if isinstance(b, int):
        if b * per_batch + k > 0:
            eng.wait_ge(sem, b * per_batch + k)
    else:
        eng.wait_ge(sem, b * per_batch + k)


def wait_alone(eng, sem, b, per_batch, k, passed):
    wait(eng, sem, b, per_batch, k)
    if not isinstance(b, int):
        eng.sem_inc(passed, 1)


def build_layer(nc, x, wq_t, wk_t, wv_t, wo_t, gate_w, w1, b1_t, w2, b2, out):
    NB, SEQ, D = x.shape
    F = wq_t.shape[1]
    NE, _, CAP = w1.shape
    DH = 64
    NH = F // DH
    NPAIR = NH // 2
    NT = SEQ // P
    NC = D // P
    NG = F // P
    HALF = NPAIR // 2
    SCALE = DH ** -0.5
    SW = P * NT * (NT + 1) // 2
    WSZ = NC * F
    assert SEQ == BANK and CAP == P and NC * F == NG * D == NE * NC * CAP == NE * D
    assert NT == 4 and NPAIR == 8 and NC == 2 and NB % 2 == 0 and NE == 8

    S_AT = [P * t * (t + 1) // 2 for t in range(NT)]
    PT_AT = {0: 0, 1: 512, 3: 896, 2: 1024}
    PT_UNITS = [((0,), 512), ((1, 3), 512), ((2,), 256)]
    SC_UNITS = [((3,), (0,)), ((2,), (0,)), ((1, 0), (0, 256))]

    AUX = 14
    K_V1, K_O1, K_XNT, K_V0, K_O0 = (0, 3, 4, 5), (1, 2), (6, 7), (8, 11, 12, 13), (9, 10)

    def aux_k(b, k):
        return 4 + k - (1 if isinstance(b, int) and b == NB - 1 and k > 8 else 0)

    aux_o1_last = AUX * (NB - 1) + aux_k(NB - 1, K_O0[1]) + 1
    aux_moe = aux_o1_last + 2

    with ExitStack() as ctx:
        def sb(name, shape, dt=F32):
            return ctx.enter_context(nc.sbuf_tensor(name, shape, dt))

        def bank(name):
            return ctx.enter_context(nc.psum_tensor(name, [P, BANK], F32))

        def sem(name):
            return ctx.enter_context(nc.semaphore(name))

        x_sb = sb("x_sb", [P, NB * NT * D])
        w_split = sb("w_split", [P, 4 * 2 * WSZ], F32R)
        xnT = sb("xnT", [P, 2, 2, NC, SEQ], F32R)
        xn = sb("xn", [P, NT, D])
        k_dup = sb("k_dup", [P, 2, 2, 2, SEQ], F32R)
        q_stk = sb("q_stk", [P, 2, 2, SEQ], F32R)
        v_sb = sb("v_sb", [P, NT, F])
        s_sb = sb("s_sb", [P, 2, SW])
        pt_sb = sb("pt_sb", [P, 2, 2, SW])
        zT = sb("zT", [P, 2, HALF, SEQ], F32R)
        mask = sb("mask", [P, SEQ])
        ident = sb("ident", [P, P])
        bn_parts = sb("bn_parts", [P, NT, 6])
        bn_mv = sb("bn_mv", [P, NT, 2])
        var_eps = sb("var_eps", [P, NT])
        rstd = sb("rstd", [P, NT])
        minus_half = sb("minus_half", [P, NT])
        euler = sb("euler", [P, NT * NE])
        neg_max = sb("neg_max", [P, 2, NT])
        row_sum = sb("row_sum", [P, 2, NT])
        row_inv = sb("row_inv", [P, 2, NT])
        b1_sb = sb("b1_sb", [P, NE])
        gate_raw = sb("gate_raw", [P, NC, NE])
        before = sb("before", [P, NE, NE])
        logit = sb("logit", [P, NT, NE])
        lmax = sb("lmax", [P, NT])
        gate = sb("gate", [P, NT, NE])
        gsum = sb("gsum", [P, NT])
        sel_pad = sb("sel_pad", [P, NT, 32])
        tok_w = sb("tok_w", [P, 2, NT])
        selT = sb("selT", [P, P], F32R)
        sel_keep = sb("sel_keep", [P, 2, NT * NE])

        def w_part(i, part):
            return w_split[:, (2 * i + part) * WSZ:(2 * i + part + 1) * WSZ]

        wk, wq, wv = ([w_part(i, r).rearrange("p (c f) -> p c f", c=NC) for r in range(2)] for i in range(3))
        wo = [w_part(3, r).rearrange("p (g d) -> p g d", g=NG) for r in range(2)]

        w1s = [w_part(0, r).rearrange("p (e c h) -> p e c h", e=NE, c=NC) for r in range(2)]
        w2s = [w_part(1, r).rearrange("p (e d) -> p e d", e=NE) for r in range(2)]
        b2s = [w_part(2, 0)[:, r * NT * D:(r + 1) * NT * D].rearrange("p (t d) -> p t d", t=NT) for r in range(2)]
        gates_w = [w_part(2, 1)[:, r * NC * NE:(r + 1) * NC * NE].rearrange("p (c e) -> p c e", c=NC) for r in range(2)]
        w1_raw = v_sb[:, :, 0:SEQ]
        w2_raw = v_sb[:, :, SEQ:F]
        b2_raw = pt_sb[:, 0, 0, 0:NT * D].rearrange("p (t d) -> p t d", t=NT)
        h_sb = [s_sb[:, r, 0:SEQ] for r in range(2)]
        h_hi = [k_dup[:, 0, r, 0, :] for r in range(2)]
        h_lo = [k_dup[:, 0, r, 1, :] for r in range(2)]
        acc = [pt_sb[:, 1, r, 0:NT * D].rearrange("p (t d) -> p t d", t=NT) for r in range(2)]
        rank_a = pt_sb[:, 0, 1, 0:256].rearrange("p (t e f) -> p t e f", t=NT, e=NE)
        rank_b = pt_sb[:, 0, 1, 256:512].rearrange("p (t e f) -> p t e f", t=NT, e=NE)
        rank = pt_sb[:, 0, 1, 512:512 + NT * NE].rearrange("p (t e) -> p t e", t=NT)

        kq_bank = bank("kq_bank")
        aux_bank = bank("aux_bank")
        sc_bank = [bank(f"sc_bank{i}") for i in range(3)]
        pt_bank = [bank(f"pt_bank{i}") for i in range(2)]
        z_bank = bank("z_bank")
        up_bank = [kq_bank, pt_bank[0]]
        y_bank = [[sc_bank[0], sc_bank[1]], [sc_bank[2], pt_bank[1]]]
        route_bank = z_bank

        d_x0 = sem("d_x0")
        d_x1 = sem("d_x1")
        d_x = sem("d_x")
        d_w = [sem(f"d_attn_w{i}") for i in range(4)]
        d_small = sem("d_small")
        d_w1, d_w2, d_b2 = sem("d_w1"), sem("d_w2"), sem("d_b2")
        d_dup = sem("d_dup")
        d_out = sem("d_out")
        const_set = sem("const_set")
        w_hi, w_lo = sem("w_hi"), sem("w_lo")
        ln_step = sem("ln_step")
        rstd_ready = sem("rstd_ready")
        pool_step = sem("pool_step")
        xn_ready = sem("xn_ready")
        aux_ready, aux_free = sem("aux_ready"), sem("aux_free")
        xn_hi = sem("xn_hi")
        xn_lo = sem("xn_lo")
        kq_ready = sem("kq_ready")
        kq_hi, kq_lo = sem("kq_hi"), sem("kq_lo")
        v_ready = sem("v_ready")
        sc_ready = sem("sc_ready")
        sc_masked = sem("sc_masked")
        exp_done = sem("exp_done")
        inv_done = sem("inv_done")
        p_ready = sem("p_ready")
        pt_ready = sem("pt_ready")
        pt_copied = sem("pt_copied")
        z_ready = sem("z_ready")
        z_hi, z_lo = sem("z_hi"), sem("z_lo")
        up_ready = sem("up_ready")
        h_ready, h_hi_ready = sem("h_ready"), sem("h_hi_ready")
        h_lo_ready = sem("h_lo_ready")
        y_ready = sem("y_ready")
        y_added = sem("y_added")
        route_ready = sem("route_ready")
        route_free = sem("route_free")
        route_step = sem("route_step")
        route_exp = sem("route_exp")
        moe_w_hi, moe_w_lo = sem("moe_w_hi"), sem("moe_w_lo")
        res_ready = sem("res_ready")
        zero_sel = sem("zero_sel")
        passed = sem("passed")

        V1_SLOTS = [(0, 1), (2, 0), (2, 1), (3, 0)]
        O1_SLOTS = [(1, 0), (1, 1)]
        XNT_SLOTS = [(3, 1), (4, 0)]
        V0_SLOTS = [(4, 1), (6, 0), (6, 1), (7, 0)]
        O0_SLOTS = [(5, 0), (5, 1)]
        STATS_SLOT, NORM_SLOT = (0, 0), (1, 0)

        def after(slot):
            p, ab = slot
            return (p, 1) if ab == 0 else (p + 1, 0)

        XNT_EXPERTS = [2, 4]
        LOGITS_AT, SELT_AT = 5, 7
        ROUTE = 12
        ROUTE_HEAD = 2

        def wait_z_used(eng, b, p):
            if p >= 0:
                wait(eng, aux_ready, b, AUX, aux_k(b, (K_O1 if p < HALF else K_O0)[1]) + 1)
            elif isinstance(b, int):
                wait(eng, aux_ready, b - 1, AUX, aux_k(b - 1, K_O0[1]) + 1)
            else:
                wait(eng, aux_ready, b, AUX, aux_k(b, K_O0[1]) + 1 - AUX)

        block = ctx.enter_context(nc.Block())

        def batches(eng, body):
            with eng.Fori(1, NB - 2, 2) as i:
                body(i, 1)
                body(i + 1, 0)

        def x_tiles(b, t, n):
            return x_sb[:, span(b * (NT * D) + t * D, n * D)]

        w_raw = [pt_sb[:, i % 2, :, 0:WSZ // 2] for i in range(2)]

        @block.sync
        def _(sp):
            sp.dma_start(x_tiles(0, 0, NT).rearrange("p (t d) -> p t d", t=NT),
                         x[0].rearrange("(t p) d -> p t d", p=P)).then_inc(d_x0, 16)
            sp.dma_start(x_tiles(1, 0, NT).rearrange("p (t d) -> p t d", t=NT),
                         x[1].rearrange("(t p) d -> p t d", p=P)).then_inc(d_x1, 16)
            weights = [w.rearrange("(c p) f -> p c f", p=P) for w in (wk_t, wq_t, wv_t)]
            for i in range(3):
                if i >= 2:
                    sp.wait_ge(w_lo, i - 1)
                sp.dma_start(w_raw[i % 2], weights[i]).then_inc(d_w[i], 16)
            sp.wait_ge(w_lo, 2)
            for c in range(2):
                sp.dma_start(w_raw[1][:, c, :].rearrange("p (g d) -> p g d", g=NG // 2),
                             wo_t[c * (F // 2):(c + 1) * (F // 2), :].rearrange("(g p) d -> p g d", p=P))\
                  .then_inc(d_w[3], 16)
            for b in range(2, NB):
                sp.dma_start(x_tiles(b, 0, NT).rearrange("p (t d) -> p t d", t=NT),
                             x[b].rearrange("(t p) d -> p t d", p=P)).then_inc(d_x, 16)
            sp.dma_start(b1_sb[:, :], b1_t).then_inc(d_small, 16)
            sp.dma_start(gate_raw[:, :, :], gate_w.rearrange("(c p) e -> p c e", p=P)).then_inc(d_small, 16)

            def duplicate(b, per, k, buf):
                wait_alone(sp, kq_lo, b, 2 * per, 2 * k + 1, passed)
                wait(sp, d_dup, b, 32 * per, 32 * k)
                for head, (src, dst) in enumerate(((0, 64), (64, 0))):
                    sp.dma_start(k_dup[dst:dst + 64, buf, head, :, :].bitcast(F32),
                                 k_dup[src:src + 64, buf, head, :, :].bitcast(F32)).then_inc(d_dup, 16)

            def batch(b, last=False):
                for p in range(NPAIR):
                    if not (last and p == NPAIR - 1):
                        duplicate(b, NPAIR, p + 1, (p + 1) % 2)

            duplicate(0, 0, 0, 0)
            batch(0)
            batches(sp, lambda b, q: batch(b))
            batch(NB - 1, last=True)

            sp.wait_ge(z_ready, NPAIR * (NB - 1) + HALF)
            for a in range(NT):
                sp.dma_start(w1_raw[:, a, :].rearrange("p (e c h) -> p e c h", e=2, c=NC),
                             w1[2 * a:2 * a + 2].rearrange("e (c p) h -> p e c h", p=P)).then_inc(d_w1, 16)
            sp.wait_ge(z_ready, NPAIR * NB)
            for a in range(NT):
                sp.dma_start(w2_raw[:, a, :].rearrange("p (e d) -> p e d", e=2),
                             w2[2 * a:2 * a + 2].rearrange("e p d -> p e d")).then_inc(d_w2, 16)
            sp.wait_ge(zero_sel, 1)
            for t in range(NT):
                sp.dma_start(b2_raw[32 * t:32 * t + NE, t, :], b2).then_inc(d_b2, 16)

            with sp.Fori(0, NB) as m:
                sp.wait_ge(res_ready, m + 1)
                sp.dma_start(out[span(m, 1)].rearrange("b (t p) d -> p (b t) d", p=P),
                             x_tiles(m, 0, NT).rearrange("p (t d) -> p t d", t=NT)).then_inc(d_out, 16)
            sp.wait_ge(d_out, 16 * NB)

        @block.gpsimd
        def _(pool):
            pool.memset(minus_half[:, :], -0.5).then_inc(const_set, 1)
            pool.memset(euler[:, :], EULER).then_inc(const_set, 1)
            pool.memset(ident[:, :], 0.0).then_inc(const_set, 1)
            pool.memset(mask[:, :], 0.0).then_inc(const_set, 1)
            pool.memset(before[:, :, :], 1.0).then_inc(const_set, 1)
            pool.memset(sel_pad[:, :, :], 0.0).then_inc(const_set, 1)
            pool.wait_ge(const_set, 6)
            pool.affine_select(out=ident[:, :], in_=ident[:, :], compare_op=ALU.not_equal, fill=1.0,
                               base=0, pattern=[[-1, P]], channel_multiplier=1).then_inc(const_set, 1)
            pool.affine_select(out=mask[:, SEQ - P:SEQ], in_=mask[:, SEQ - P:SEQ], compare_op=ALU.is_ge,
                               fill=-NEG, base=0, pattern=[[-1, P]], channel_multiplier=1).then_inc(const_set, 1)
            pool.affine_select(out=before[:, :, :], in_=before[:, :, :], compare_op=ALU.is_ge, fill=0.0,
                               base=-1, pattern=[[1, NE], [-1, NE]], channel_multiplier=0).then_inc(const_set, 1)

            def rsqrt(c, k):
                wait_alone(pool, ln_step, c, 2, 2 * k + 2, passed)
                pool.tensor_scalar(var_eps[:, :], bn_mv[:, :, 1], EPS, None, ALU.add).then_inc(pool_step, 1)
                wait(pool, pool_step, c, 1, k + 1)
                pool.tensor_tensor(rstd[:, :], var_eps[:, :], minus_half[:, :], ALU.pow).then_inc(rstd_ready, 1)

            rsqrt(0, 0)
            rsqrt(0, 1)
            batches(pool, lambda b, q: rsqrt(b, 1))
            rsqrt(NB, 0)

            pool.wait_ge(pt_copied, 3 * NH * NB)
            pool.wait_ge(z_ready, NPAIR * NB)
            pool.memset(b2_raw, 0.0).then_inc(zero_sel, 1)

            def lo_part(m, e):
                wait(pool, h_hi_ready, m, NE, e + 1)
                wait(pool, y_ready, m, NE, e - 1)
                pool.tensor_tensor(h_lo[e % 2], h_sb[e % 2], h_hi[e % 2].bitcast(F32), ALU.subtract)\
                    .then_inc(h_lo_ready, 1)

            def route_exp_part(m, k):
                wait(pool, route_step, m, ROUTE, ROUTE * k + ROUTE_HEAD)
                pool.tensor_tensor(gate[:, :, :].rearrange("p t e -> p (t e)"), euler[:, :],
                                   logit[:, :, :].rearrange("p t e -> p (t e)"), ALU.pow).then_inc(route_exp, 1)

            def experts(m, last=False):
                for e in range(NE):
                    if e == 1 and not last:
                        rsqrt(m, NB + 1)
                    lo_part(m, e)
                    if e == LOGITS_AT and not last:
                        route_exp_part(m, 1)

            route_exp_part(0, 0)
            experts(0)
            batches(pool, lambda m, q: experts(m))
            experts(NB - 1, last=True)

        @block.scalar
        def _(act):
            def weight_hi(i, src, dst, landed, count, done):
                act.wait_ge(landed, count)
                act.activation(dst, src, ACT.Copy).then_inc(done, 1)

            def xnt_hi(b, per, k, u, buf):
                wait(act, aux_ready, b, per, k + 1)
                act.activation(xnT[:, buf, 0, u, :], aux_bank[:, :], ACT.Copy).then_inc(xn_hi, 1)

            def v_unit(b, k, half, t):
                wait(act, aux_ready, b, AUX, aux_k(b, k) + 1)
                act.activation(v_sb[:, t, half * SEQ:(half + 1) * SEQ], aux_bank[:, :], ACT.Copy)\
                   .then_inc(aux_free, 1)

            def k_hi(b, p, buf):
                wait(act, kq_ready, b, 2 * NPAIR, 2 * p + 1)
                wait(act, d_dup, b, 32 * NPAIR, 32 * (p - 1))
                for head in range(2):
                    r = slice(64 * head, 64 * head + 64)
                    last = act.activation(k_dup[r, buf, head, 0, :], kq_bank[r, :], ACT.Copy)
                last.then_inc(kq_hi, 1)

            def q_hi(b, p, buf):
                wait(act, kq_ready, b, 2 * NPAIR, 2 * p + 2)
                for head in range(2):
                    r = slice(64 * head, 64 * head + 64)
                    last = act.activation(q_stk[r, buf, head, :], kq_bank[r, :], ACT.Copy)
                last.then_inc(kq_hi, 1)

            def exps(b, h, order):
                for t in order:
                    wait(act, sc_masked, b, 4 * NH, 4 * h + NT - t)
                    s = s_sb[:, h % 2, S_AT[t]:S_AT[t] + P * (t + 1)]
                    act.activation(s, s, ACT.Exp, bias=neg_max[:, h % 2, t:t + 1], scale=-1.0,
                                   accum_out=row_sum[:, h % 2, t:t + 1]).then_inc(exp_done, 1)

            def pt_copy(b, h, unit):
                n = 3 * h + unit
                wait(act, pt_ready, b, 3 * NH, n + 1)
                tiles, width = PT_UNITS[unit]
                at = PT_AT[tiles[0]]
                pair = h // 2
                if unit == 0:
                    wait(act, z_ready, b, NPAIR, pair - 1)
                act.activation(pt_sb[:, pair % 2, h % 2, at:at + width], pt_bank[n % 2][:, 0:width], ACT.Copy)\
                   .then_inc(pt_copied, 1)

            def z_part(b, p):
                wait(act, z_ready, b, NPAIR, p + 1)
                wait_z_used(act, b, p)
                act.activation(zT[:, 0, p % HALF, :], z_bank[:, :], ACT.Copy).then_inc(z_hi, 1)

            def batch(b, q, first=False, last=False):
                for p in range(NPAIR):
                    for ab in range(2):
                        h = 2 * p + ab
                        slot = (p, ab)
                        if ab == 0 and not (first and p < 2):
                            z_part(b, p - 2)
                        if not (last and p == NPAIR - 1):
                            (k_hi if ab == 0 else q_hi)(b, p + 1, (p + 1) % 2)
                        for half, slots, ks in ((1, V1_SLOTS, K_V1), (0, V0_SLOTS, K_V0)):
                            for t in range(NT):
                                skip = (last and half == 0) or (first and half == 1 and t < 2)
                                if slot == after(slots[t]) and not skip:
                                    v_unit(b, ks[t], half, t)
                        for u in range(NC):
                            if slot == after(XNT_SLOTS[u]):
                                xnt_hi(b, AUX, aux_k(b, K_XNT[u]), u, 1 - q)
                        has_prev = not (first and h == 0)
                        exps(b, h, (3,))
                        if has_prev:
                            pt_copy(b, h - 1, 0)
                        exps(b, h, (2,))
                        if has_prev:
                            pt_copy(b, h - 1, 1)
                        exps(b, h, (1, 0))
                        if has_prev:
                            pt_copy(b, h - 1, 2)
                        if last and slot == (NPAIR - 1, 0):
                            weight_hi(0, w1_raw, w_part(0, 0).rearrange("p (a n) -> p a n", a=NT), d_w1, 16 * NT,
                                      moe_w_hi)

            for i in range(2):
                weight_hi(i, w_raw[i % 2], w_part(i, 0).rearrange("p (c f) -> p c f", c=2), d_w[i], 16, w_hi)
            for u in range(NC):
                xnt_hi(0, 0, u, u, 0)
            weight_hi(2, w_raw[0], w_part(2, 0).rearrange("p (c f) -> p c f", c=2), d_w[2], 16, w_hi)
            k_hi(0, 0, 0)
            q_hi(0, 0, 0)
            weight_hi(3, w_raw[1], w_part(3, 0).rearrange("p (c f) -> p c f", c=2), d_w[3], 32, w_hi)
            for t in range(NT):
                v_unit(0, t - 2, 0, t)
            for t in range(2):
                v_unit(0, 2 + t, 1, t)
            batch(0, 0, first=True)
            batches(act, lambda b, q: batch(b, q))
            batch(NB - 1, 1, last=True)
            z_part(NB, -2)
            for unit in range(3):
                pt_copy(NB, -1, unit)
            z_part(NB, -1)

            act.wait_ge(aux_free, aux_moe)
            weight_hi(2, gate_raw[:, :, :], gates_w[0], d_small, 32, moe_w_hi)
            weight_hi(1, w2_raw, w_part(1, 0).rearrange("p (a n) -> p a n", a=NT), d_w2, 16 * NT, moe_w_hi)
            weight_hi(2, b2_raw, b2s[0], d_b2, 16 * NT, moe_w_hi)

            def selT_copy(m, k):
                wait(act, route_ready, m, 4, 4 * k + 2)
                act.activation(selT[:, :], route_bank[:, 0:P], ACT.Copy).then_inc(route_free, 1)

            def bias_part(m, k, q, u):
                wait(act, route_ready, m, 4, 4 * k + 3 + u)
                wait(act, res_ready, m, 1, k - 1)
                act.activation(acc[q][:, 2 * u:2 * u + 2, :],
                               route_bank[:, :].rearrange("p (t d) -> p t d", t=2), ACT.Copy)\
                   .then_inc(route_free, 1)

            def gelu(m, e):
                wait(act, up_ready, m, NE, e + 1)
                wait(act, h_lo_ready, m, NE, e - 1)
                act.activation(h_sb[e % 2], up_bank[e % 2][:, :], ACT.Gelu, bias=b1_sb[:, e:e + 1])\
                   .then_inc(h_ready, 1)
                wait(act, h_ready, m, NE, e + 1)
                wait(act, y_ready, m, NE, e - 1)
                act.activation(h_hi[e % 2], h_sb[e % 2], ACT.Copy).then_inc(h_hi_ready, 1)

            def experts(m, q, first=False, last=False):
                for e in range(NE):
                    gelu(m, e)
                    if not last and e in XNT_EXPERTS:
                        u = XNT_EXPERTS.index(e)
                        xnt_hi(m, 2, aux_moe + u, u, 1 - q)
                    if not last and e == SELT_AT:
                        selT_copy(m, 1)
                        bias_part(m, 1, 1 - q, 0)
                    if not first and e == 0:
                        bias_part(m, 0, q, 1)

            selT_copy(0, 0)
            bias_part(0, 0, 0, 0)
            bias_part(0, 0, 0, 1)
            experts(0, 0, first=True)
            batches(act, lambda m, q: experts(m, q))
            experts(NB - 1, 1, last=True)

        @block.vector
        def _(dve):
            def weight_lo(src, hi, dst, ready, count, done):
                dve.wait_ge(ready, count)
                dve.tensor_tensor(dst, src, hi.bitcast(F32), ALU.subtract).then_inc(done, 1)

            def stats(c, k, b):
                for t in range(NT):
                    last = dve.bn_stats(bn_parts[:, t, :], x_tiles(b, t, 1))
                last.then_inc(ln_step, 1)
                wait_alone(dve, ln_step, c, 2, 2 * k + 1, passed)
                for t in range(NT):
                    last = dve.bn_aggr(bn_mv[:, t, :], bn_parts[:, t, :])
                last.then_inc(ln_step, 1)

            def normalise(c, k, b, aux, ka):
                wait(dve, rstd_ready, c, 1, k + 1)
                wait(dve, aux_ready, *aux, ka)
                for t in range(NT):
                    last = dve.tensor_scalar(xn[:, t, :], x_tiles(b, t, 1), bn_mv[:, t, 0:1],
                                             rstd[:, t:t + 1], ALU.subtract, ALU.mult)
                last.then_inc(xn_ready, 1)

            def xnt_lo(c, k, u, buf):
                wait(dve, xn_hi, c, 2, 2 * k + u + 1)
                dve.tensor_tensor(xnT[:, buf, 1, u, :], aux_bank[:, :], xnT[:, buf, 0, u, :].bitcast(F32),
                                  ALU.subtract).then_inc(aux_free, 1)

            def k_lo(b, p, buf):
                wait(dve, kq_hi, b, 2 * NPAIR, 2 * p + 1)
                for head in range(2):
                    r = slice(64 * head, 64 * head + 64)
                    last = dve.tensor_tensor(k_dup[r, buf, head, 1, :], kq_bank[r, :],
                                             k_dup[r, buf, head, 0, :].bitcast(F32), ALU.subtract)
                last.then_inc(kq_lo, 1)

            def q_lo(b, p, buf):
                wait(dve, kq_hi, b, 2 * NPAIR, 2 * p + 2)
                for head in range(2):
                    r = slice(64 * head, 64 * head + 64)
                    o = slice(64 - 64 * head, 128 - 64 * head)
                    last = dve.tensor_tensor(q_stk[o, buf, head, :], kq_bank[r, :],
                                             q_stk[r, buf, head, :].bitcast(F32), ALU.subtract)
                last.then_inc(kq_lo, 1)

            def mask_and_max(b, h):
                wait(dve, pt_ready, b, 3 * NH, 3 * (h - 1))
                for unit, (tiles, cols) in enumerate(SC_UNITS):
                    wait_alone(dve, sc_ready, b, 3 * NH, 3 * h + unit + 1, passed)
                    for t, at in zip(tiles, cols):
                        n = P * (t + 1)
                        dve.tensor_tensor_reduce(
                            out=s_sb[:, h % 2, S_AT[t]:S_AT[t] + n], in0=sc_bank[unit][:, at:at + n],
                            in1=mask[:, SEQ - n:SEQ], scale=-SCALE, scalar=FLT_MAX, op0=ALU.add, op1=ALU.min,
                            accum_out=neg_max[:, h % 2, t:t + 1]).then_inc(sc_masked, 1)

            def divide(b, h):
                for i, (lo_t, hi_t) in enumerate(((2, 4), (0, 2))):
                    wait(dve, exp_done, b, 4 * NH, 4 * h + 2 * i + 2)
                    dve.reciprocal(row_inv[:, h % 2, lo_t:hi_t], row_sum[:, h % 2, lo_t:hi_t]).then_inc(inv_done, 1)
                    wait(dve, inv_done, b, 2 * NH, 2 * h + i + 1)
                    for t in (hi_t - 1, lo_t):
                        s = s_sb[:, h % 2, S_AT[t]:S_AT[t] + P * (t + 1)]
                        last = dve.tensor_scalar(s, s, row_inv[:, h % 2, t:t + 1], None, ALU.mult)
                    last.then_inc(p_ready, 1)

            def z_part(b, p):
                wait(dve, z_hi, b, NPAIR, p + 1)
                dve.tensor_tensor(zT[:, 1, p % HALF, :], z_bank[:, :], zT[:, 0, p % HALF, :].bitcast(F32),
                                  ALU.subtract).then_inc(z_lo, 1)

            def add_output(b, k, b_x, u):
                wait(dve, aux_ready, b, AUX, aux_k(b, k) + 1)
                dve.tensor_tensor(x_tiles(b_x, 2 * u, 2), x_tiles(b_x, 2 * u, 2), aux_bank[:, :], ALU.add)\
                   .then_inc(aux_free, 1)

            def batch(b, q, first=False, last=False):
                for p in range(NPAIR):
                    for ab in range(2):
                        h = 2 * p + ab
                        slot = (p, ab)
                        mask_and_max(b, h)
                        if ab == 0 and not (first and p < 2):
                            z_part(b, p - 2)
                        for slots, ks, b_x in ((O1_SLOTS, K_O1, b - 1), (O0_SLOTS, K_O0, b)):
                            for u in range(2):
                                if slot == after(slots[u]) and not (first and slots == O1_SLOTS):
                                    add_output(b, ks[u], b_x, u)
                        for u in range(NC):
                            if slot == after(XNT_SLOTS[u]):
                                xnt_lo(b, 1, u, 1 - q)
                        if not (last and p == NPAIR - 1):
                            (k_lo if ab == 0 else q_lo)(b, p + 1, (p + 1) % 2)
                        divide(b, h)
                        b_next = 0 if last else b + 1
                        if slot == STATS_SLOT:
                            if first:
                                dve.wait_ge(d_x1, 16)
                            stats(b, 1, b_next)
                        if slot == NORM_SLOT:
                            normalise(b, 1, b_next, (b, AUX), aux_k(0, K_XNT[1]) + 1 - AUX)
                            if first:
                                dve.wait_ge(d_x, 16 * (NB - 2))
                        if last and slot == (NPAIR - 1, 0):
                            weight_lo(w1_raw, w_part(0, 0).rearrange("p (a n) -> p a n", a=NT),
                                      w_part(0, 1).rearrange("p (a n) -> p a n", a=NT), moe_w_hi, 1, moe_w_lo)

            dve.wait_ge(d_x0, 16)
            stats(0, 0, 0)
            normalise(0, 0, 0, (0, 0), 0)
            for i in range(2):
                weight_lo(w_raw[i], w_part(i, 0).rearrange("p (c f) -> p c f", c=2),
                          w_part(i, 1).rearrange("p (c f) -> p c f", c=2), w_hi, i + 1, w_lo)
            for u in range(NC):
                xnt_lo(0, 0, u, 0)
            weight_lo(w_raw[0], w_part(2, 0).rearrange("p (c f) -> p c f", c=2),
                      w_part(2, 1).rearrange("p (c f) -> p c f", c=2), w_hi, 3, w_lo)
            k_lo(0, 0, 0)
            q_lo(0, 0, 0)
            weight_lo(w_raw[1], w_part(3, 0).rearrange("p (c f) -> p c f", c=2),
                      w_part(3, 1).rearrange("p (c f) -> p c f", c=2), w_hi, 4, w_lo)
            dve.wait_ge(const_set, 9)
            batch(0, 0, first=True)
            batches(dve, lambda b, q: batch(b, q))
            batch(NB - 1, 1, last=True)
            z_part(NB, -2)
            z_part(NB, -1)
            for u in range(2):
                dve.wait_ge(aux_ready, aux_o1_last + u + 1)
                dve.tensor_tensor(x_tiles(NB - 1, 2 * u, 2), x_tiles(NB - 1, 2 * u, 2), aux_bank[:, :], ALU.add)\
                   .then_inc(aux_free, 1)

            weight_lo(gate_raw[:, :, :], gates_w[0], gates_w[1], moe_w_hi, 2, moe_w_lo)
            weight_lo(w2_raw, w_part(1, 0).rearrange("p (a n) -> p a n", a=NT),
                      w_part(1, 1).rearrange("p (a n) -> p a n", a=NT), moe_w_hi, 3, moe_w_lo)
            weight_lo(b2_raw, b2s[0], b2s[1], moe_w_hi, 4, moe_w_lo)

            def linker(m, k, first):
                step = [first]

                def link(ins):
                    step[0] += 1
                    ins.then_inc(route_step, 1)
                    wait(dve, route_step, m, ROUTE, ROUTE * k + step[0])

                return link, step

            def route_head(m, k):
                link, step = linker(m, k, 0)
                lg = route_bank[:, 0:NT * NE].rearrange("p (t e) -> p t e", t=NT)
                tile_bc = [P, NT, NE]
                wait(dve, route_ready, m, 4, 4 * k + 1)
                link(dve.tensor_reduce(lmax[:, :], lg, AX.X, ALU.max))
                ins = dve.tensor_tensor(logit[:, :, :], lg, lmax[:, :].unsqueeze(2).broadcast_to(tile_bc), ALU.subtract)
                link(ins)
                assert step[0] == ROUTE_HEAD

            def route_tail(m, k, q):
                link, step = linker(m, k, ROUTE_HEAD)
                tile_bc = [P, NT, NE]
                wait(dve, route_exp, m, 1, k + 1)
                link(dve.tensor_reduce(gsum[:, :], gate[:, :, :], AX.X, ALU.add))
                link(dve.reciprocal(gsum[:, :], gsum[:, :]))
                link(dve.tensor_tensor(gate[:, :, :], gate[:, :, :], gsum[:, :].unsqueeze(2).broadcast_to(tile_bc), ALU.mult))
                other = gate[:, :, :].unsqueeze(2).broadcast_to([P, NT, NE, NE])
                own = gate[:, :, :].unsqueeze(3).broadcast_to([P, NT, NE, NE])
                dve.tensor_tensor(rank_a, other, own, ALU.is_gt)
                link(dve.tensor_tensor(rank_b, other, own, ALU.is_equal))
                link(dve.tensor_tensor(rank_b, rank_b, before[:, :, :].unsqueeze(1).broadcast_to([P, NT, NE, NE]),
                                       ALU.mult))
                link(dve.tensor_tensor(rank_a, rank_a, rank_b, ALU.add))
                link(dve.tensor_reduce(rank, rank_a, AX.X, ALU.add))
                wait(dve, route_ready, m, 4, 4 * k - 2)
                dve.tensor_scalar(sel_keep[:, q, :].rearrange("p (t e) -> p t e", t=NT), rank, 1.5, None, ALU.is_lt)
                link(dve.tensor_scalar(sel_pad[:, :, 0:NE], rank, 1.5, None, ALU.is_lt))
                link(dve.tensor_tensor(gate[:, :, :], gate[:, :, :], sel_pad[:, :, 0:NE], ALU.mult))
                link(dve.tensor_reduce(tok_w[:, q, :], gate[:, :, :], AX.X, ALU.add))
                assert step[0] == ROUTE

            def sum_expert(m, e, q):
                if e == 0:
                    wait(dve, route_free, m, 3, 3)
                for u in range(2):
                    if u == 0:
                        wait(dve, y_ready, m, NE, e + 1)
                    wait(dve, y_added, m, 2 * NE, 2 * e + u - 1)
                    for t in (2 * u, 2 * u + 1):
                        last = dve.scalar_tensor_tensor(
                            acc[q][:, t, :], y_bank[e % 2][u][:, (t % 2) * D:(t % 2) * D + D],
                            sel_keep[:, q, t * NE + e:t * NE + e + 1], acc[q][:, t, :], ALU.mult, ALU.add)
                    last.then_inc(y_added, 1)

            def result(m, q):
                wait(dve, y_added, m, 2 * NE, 2 * NE)
                for t in range(NT):
                    last = dve.scalar_tensor_tensor(x_tiles(m, t, 1), acc[q][:, t, :], tok_w[:, q, t:t + 1],
                                                    x_tiles(m, t, 1), ALU.mult, ALU.add)
                last.then_inc(res_ready, 1)

            def experts(m, q, last=False):
                for e in range(NE):
                    if not last and e == 0:
                        stats(m, NB + 1, m + 1)
                    sum_expert(m, e, q)
                    if not last and e == 0:
                        normalise(m, NB + 1, m + 1, (m, 2), aux_moe)
                    if not last and e == 1:
                        xnt_lo(m, NB + 1, 0, 1 - q)
                    if not last and e == 2:
                        xnt_lo(m, NB + 1, 1, 1 - q)
                    if not last and e == 3:
                        route_head(m, 1)
                    if not last and e == 4:
                        route_tail(m, 1, 1 - q)
                result(m, q)

            route_head(0, 0)
            route_tail(0, 0, 0)
            experts(0, 0)
            batches(dve, lambda m, q: experts(m, q))
            experts(NB - 1, 1, last=True)

        @block.tensor
        def _(pe):
            def split_product(out_ap, pairs):
                terms = [(s[i], v[j]) for s, v in pairs for i, j in ((0, 0), (0, 1), (1, 0))]
                for n, (s, v) in enumerate(terms):
                    last = pe.matmul(out_ap, s, v, start=(n == 0), stop=(n == len(terms) - 1))
                return last

            def k_or_q(b, p, w, unit, buf, cols):
                wait(pe, kq_lo, b, 2 * NPAIR, 2 * p + unit)
                split_product(kq_bank[:, :],
                              [([w[r][:, c, cols * P:(cols + 1) * P] for r in range(2)],
                                [xnT[:, buf, r, c, :] for r in range(2)]) for c in range(NC)]).then_inc(kq_ready, 1)

            def v_unit(b, k, half, t, buf):
                wait_aux(b, k)
                split_product(aux_bank[:, :],
                              [([xnT[:, buf, r, c, t * P:(t + 1) * P] for r in range(2)],
                                [wv[r][:, c, half * SEQ:(half + 1) * SEQ] for r in range(2)]) for c in range(NC)])\
                    .then_inc(aux_ready, 1)

            def wait_aux(b, k):
                wait(pe, aux_free, b, AUX, aux_k(b, k))

            def xnt_unit(u):
                for t in range(NT):
                    last = pe.transpose(aux_bank[:, t * P:(t + 1) * P], xn[:, t, u * P:(u + 1) * P], ident[:, :])
                last.then_inc(aux_ready, 1)

            def output_unit(u, half):
                for t in (2 * u, 2 * u + 1):
                    last = split_product(aux_bank[:, (t % 2) * D:(t % 2) * D + D],
                                         [([zT[:, r, g, t * P:(t + 1) * P] for r in range(2)],
                                           [wo[r][:, half * HALF + g, :] for r in range(2)]) for g in range(HALF)])
                last.then_inc(aux_ready, 1)

            def scores(b, h):
                p, head = h // 2, h % 2
                if head == 0:
                    wait(pe, kq_lo, b, 2 * NPAIR, 2 * p + 2)
                    wait(pe, d_dup, b, 32 * NPAIR, 32 * (p + 1))
                for unit, (tiles, cols) in enumerate(SC_UNITS):
                    wait(pe, sc_masked, b, 4 * NH, 4 * (h - 1) + (1, 2, 4)[unit])
                    for t, at in zip(tiles, cols):
                        n = P * (t + 1)
                        for part in range(2):
                            last = pe.matmul(sc_bank[unit][:, at:at + n],
                                             q_stk[:, p % 2, head, t * P:(t + 1) * P],
                                             k_dup[:, p % 2, head, part, 0:n], start=(part == 0), stop=(part == 1))
                    last.then_inc(sc_ready, 1)

            def transposes(b, h, units):
                wait(pe, p_ready, b, 2 * NH, 2 * (h + 1))
                for unit in units:
                    n = 3 * h + unit
                    wait(pe, pt_copied, b, 3 * NH, n - 1)
                    at = 0
                    for j in PT_UNITS[unit][0]:
                        for t in range(j, NT):
                            col = S_AT[t] + j * P
                            last = pe.transpose(pt_bank[n % 2][:, at:at + P], s_sb[:, h % 2, col:col + P], ident[:, :])
                            at += P
                    last.then_inc(pt_ready, 1)

            def head_outputs(b, p, keys):
                wait(pe, pt_copied, b, 3 * NH, 6 * p + 4 if keys[0] == 0 else 6 * p + 6)
                if keys[0] == 0:
                    wait(pe, z_lo, b, NPAIR, p)
                    if p == 0:
                        wait(pe, aux_free, b, AUX, 8 if isinstance(b, int) and b == 0 else 4)
                    if p == HALF:
                        wait_aux(b, K_V1[3] + 1)
                for j in keys:
                    for head in range(2):
                        n = SEQ - j * P
                        f = (2 * p + head) % NH * DH
                        last = pe.matmul(z_bank[64 * head:64 * head + 64, j * P:SEQ], v_sb[:, j, f:f + DH],
                                         pt_sb[:, p % 2, head, PT_AT[j]:PT_AT[j] + n],
                                         start=(j == 0), stop=(j == NT - 1))
                if keys[-1] == NT - 1:
                    last.then_inc(z_ready, 1)

            def batch(b, q, first=False, last=False):
                for p in range(NPAIR):
                    for ab in range(2):
                        h = 2 * p + ab
                        slot = (p, ab)
                        scores(b, h)
                        if not (first and h == 0):
                            transposes(b, h - 1, (0, 1))
                        if ab == 1 and not (first and p == 0):
                            head_outputs(b, p - 1, (1, 2, 3))
                        for half, slots, ks in ((1, V1_SLOTS, K_V1), (0, V0_SLOTS, K_V0)):
                            for t in range(NT):
                                skip = (last and half == 0) or (first and half == 1 and t < 2)
                                if slot == slots[t] and not skip:
                                    v_unit(b, ks[t], half, t, 1 - q if half == 0 else q)
                        for u in range(NC):
                            if slot == XNT_SLOTS[u]:
                                wait(pe, xn_ready, b, 1, 2)
                                wait_aux(b, K_XNT[u])
                                xnt_unit(u)
                        if not (first and h == 0):
                            transposes(b, h - 1, (2,))
                        if ab == 0 and not (first and p == 0):
                            head_outputs(b, p - 1, (0,))
                        for half, slots, ks in ((1, O1_SLOTS, K_O1), (0, O0_SLOTS, K_O0)):
                            for u in range(2):
                                if slot == slots[u] and not (first and half == 1):
                                    wait(pe, z_lo, b, NPAIR, HALF * (1 - half))
                                    wait_aux(b, ks[u])
                                    output_unit(u, half)
                        pair = p + 1 + ab
                        if not (last and pair >= NPAIR):
                            k_or_q(b, pair, (wq, wk)[ab], 1 - ab, q if pair < NPAIR else 1 - q, pair % NPAIR)

            pe.wait_ge(const_set, 7)
            pe.wait_ge(xn_ready, 1)
            for u in range(NC):
                wait(pe, aux_free, 0, 0, u)
                xnt_unit(u)
            pe.wait_ge(aux_free, NC)
            pe.wait_ge(w_lo, 1)
            k_or_q(0, 0, wk, 0, 0, 0)
            pe.wait_ge(w_lo, 2)
            k_or_q(0, 0, wq, 1, 0, 0)
            k_or_q(0, 1, wk, 0, 0, 1)
            pe.wait_ge(w_lo, 3)
            for t in range(NT):
                v_unit(0, t - 2, 0, t, 0)
            for t in range(2):
                v_unit(0, 2 + t, 1, t, 0)
            pe.wait_ge(w_lo, 4)
            batch(0, 0, first=True)
            batches(pe, lambda b, q: batch(b, q))
            batch(NB - 1, 1, last=True)
            transposes(NB, -1, (0, 1, 2))
            head_outputs(NB, -1, (0,))
            head_outputs(NB, -1, (1, 2, 3))
            for u in range(2):
                pe.wait_ge(z_lo, NPAIR * NB)
                pe.wait_ge(aux_free, aux_o1_last + u)
                output_unit(u, 1)

            def logits_unit(m, k, buf):
                wait(pe, route_free, m, 3, 3 * k)
                wait(pe, aux_free, m, 2, aux_moe + 2 * (k - 1) + 2)
                for t in range(NT):
                    last = split_product(route_bank[:, t * NE:(t + 1) * NE],
                                         [([xnT[:, buf, r, c, t * P:(t + 1) * P] for r in range(2)],
                                           [gates_w[r][:, c, :] for r in range(2)]) for c in range(NC)])
                last.then_inc(route_ready, 1)

            def selT_unit(m, k):
                wait(pe, route_step, m, ROUTE, ROUTE * k + 10)
                pe.transpose(route_bank[:, 0:P], sel_pad[:, :, :].rearrange("p t e -> p (t e)"), ident[:, :])\
                  .then_inc(route_ready, 1)

            def bias_unit(m, k, u):
                wait(pe, route_free, m, 3, 3 * k + 1 + u)
                for t in (2 * u, 2 * u + 1):
                    for r in range(2):
                        last = pe.matmul(route_bank[:, (t % 2) * D:(t % 2) * D + D], selT[:, :], b2s[r][:, t, :],
                                         start=(r == 0), stop=(r == 1))
                last.then_inc(route_ready, 1)

            def up(m, e, q):
                wait(pe, h_ready, m, NE, e - 1)
                split_product(up_bank[e % 2][:, :],
                              [([w1s[r][:, e, c, :] for r in range(2)],
                                [xnT[:, q, r, c, :] for r in range(2)]) for c in range(NC)]).then_inc(up_ready, 1)

            def down(m, e):
                wait(pe, h_lo_ready, m, NE, e + 1)
                for u in range(2):
                    wait(pe, y_added, m, 2 * NE, 2 * (e - 2) + u + 1)
                    for t in (2 * u, 2 * u + 1):
                        last = split_product(y_bank[e % 2][u][:, (t % 2) * D:(t % 2) * D + D],
                                             [([h_hi[e % 2][:, t * P:(t + 1) * P], h_lo[e % 2][:, t * P:(t + 1) * P]],
                                               [w2s[r][:, e % NE, :] for r in range(2)])])
                last.then_inc(y_ready, 1)

            def experts(m, q, first=False, last=False):
                for e in range(NE):
                    up(m, e, q)
                    if not last and e in XNT_EXPERTS:
                        u = XNT_EXPERTS.index(e)
                        wait(pe, xn_ready, m, 1, NB + 2)
                        wait(pe, aux_free, m, 2, aux_moe + u)
                        xnt_unit(u)
                    if not last and e == LOGITS_AT:
                        logits_unit(m, 1, 1 - q)
                    if not last and e == SELT_AT:
                        selT_unit(m, 1)
                    if not first and e == 0:
                        bias_unit(m, 0, 1)
                    if not (first and e == 0):
                        down(m, e - 1)
                    if not last and e == SELT_AT:
                        bias_unit(m, 1, 0)

            pe.wait_ge(aux_free, aux_moe)
            pe.wait_ge(moe_w_lo, 2)
            logits_unit(0, 0, 0)
            pe.wait_ge(moe_w_lo, 4)
            selT_unit(0, 0)
            bias_unit(0, 0, 0)
            bias_unit(0, 0, 1)
            experts(0, 0, first=True)
            batches(pe, lambda m, q: experts(m, q))
            experts(NB - 1, 1, last=True)
            down(NB, -1)


def kernel(L0_attn_x, L0_attn_W_K, L0_attn_W_Q, L0_attn_W_V, L0_attn_W_O, L0_ffn_gate_w,
           L0_ffn_w1, L0_ffn_b1, L0_ffn_w2, L0_ffn_b2):
    import numpy as np
    import concourse.bacc as bacc
    from concourse.bass_utils import run_bass_kernel_spmd

    def rows(w):
        w = np.asarray(w)
        return np.ascontiguousarray(w.reshape(-1, w.shape[-1]).T)

    arrays = {
        "x": np.ascontiguousarray(L0_attn_x),
        "wq_t": rows(L0_attn_W_Q),
        "wk_t": rows(L0_attn_W_K),
        "wv_t": rows(L0_attn_W_V),
        "wo_t": np.ascontiguousarray(np.asarray(L0_attn_W_O).T),
        "gate_w": np.ascontiguousarray(L0_ffn_gate_w),
        "w1": np.ascontiguousarray(L0_ffn_w1),
        "b1_t": np.ascontiguousarray(np.asarray(L0_ffn_b1).T),
        "w2": np.ascontiguousarray(L0_ffn_w2),
        "b2": np.ascontiguousarray(L0_ffn_b2),
    }
    nc = bacc.Bacc("TRN2", target_bir_lowering=False, num_devices=1)
    args = {k: nc.dram_tensor(k, a.shape, mybir.dt.from_np(a.dtype), kind="ExternalInput").ap()
            for k, a in arrays.items()}
    y = nc.dram_tensor("y", arrays["x"].shape, F32, kind="ExternalOutput").ap()
    build_layer(nc, out=y, **args)
    r = run_bass_kernel_spmd(nc, [arrays], core_ids=[0])
    return r.results[0]["y"]
```

```python
from contextlib import ExitStack

import concourse.bass as bass
from concourse import mybir

ALU = mybir.AluOpType
ACT = mybir.ActivationFunctionType
AX = mybir.AxisListType
F32 = mybir.dt.float32
F32R = mybir.dt.float32r

P = 128
BANK = 512
NEG = 10000000000.0
EPS = 1e-5
EULER = 2.718281828459045
FLT_MAX = 3.4028234e38


def span(start, size):
    return bass.ds(start, size)


def wait(eng, sem, b, per_batch, k):
    if isinstance(b, int):
        if b * per_batch + k > 0:
            eng.wait_ge(sem, b * per_batch + k)
    else:
        eng.wait_ge(sem, b * per_batch + k)


def wait_alone(eng, sem, b, per_batch, k, passed):
    wait(eng, sem, b, per_batch, k)
    if not isinstance(b, int):
        eng.sem_inc(passed, 1)


def build_layer(nc, x, wq_t, wk_t, wv_t, wo_t, gate_w, w1, b1_t, w2, b2, out):
    NB, SEQ, D = x.shape
    F = wq_t.shape[1]
    NE, _, CAP = w1.shape
    DH = 64
    NH = F // DH
    NPAIR = NH // 2
    NT = SEQ // P
    NC = D // P
    NG = F // P
    HALF = NPAIR // 2
    SCALE = DH ** -0.5
    SW = P * NT * (NT + 1) // 2
    WSZ = NC * F
    assert SEQ == BANK and CAP == P and NC * F == NG * D == NE * NC * CAP == NE * D
    assert NT == 4 and NPAIR == 8 and NC == 2 and NB % 2 == 0 and NE == 8

    S_AT = [P * t * (t + 1) // 2 for t in range(NT)]
    PT_AT = {0: 0, 1: 512, 3: 896, 2: 1024}
    PT_UNITS = [((0,), 512), ((1, 3), 512), ((2,), 256)]
    SC_UNITS = [((3,), (0,)), ((2,), (0,)), ((1, 0), (0, 256))]

    AUX = 14
    K_V1, K_O1, K_XNT, K_V0, K_O0 = (0, 3, 4, 5), (1, 2), (6, 7), (8, 11, 12, 13), (9, 10)

    def aux_k(b, k):
        if isinstance(b, int) and b == 0 and 0 <= k < 4:
            return 6 + (k == 3)
        return 4 + k - (1 if isinstance(b, int) and b == NB - 1 and k > 8 else 0)

    aux_o1_last = AUX * (NB - 1) + aux_k(NB - 1, K_O0[1]) + 1
    aux_moe = aux_o1_last + 2

    with ExitStack() as ctx:
        def sb(name, shape, dt=F32):
            return ctx.enter_context(nc.sbuf_tensor(name, shape, dt))

        def bank(name):
            return ctx.enter_context(nc.psum_tensor(name, [P, BANK], F32))

        def sem(name):
            return ctx.enter_context(nc.semaphore(name))

        x_sb = sb("x_sb", [P, NB * NT * D])
        w_split = sb("w_split", [P, 4 * 2 * WSZ], F32R)
        xnT = sb("xnT", [P, 2, 2, NC, SEQ], F32R)
        xn = sb("xn", [P, NT, D])
        k_dup = sb("k_dup", [P, 2, 2, 2, SEQ], F32R)
        q_stk = sb("q_stk", [P, 2, 2, SEQ], F32R)
        v_sb = sb("v_sb", [P, NT, F])
        s_sb = sb("s_sb", [P, 2, SW])
        pt_sb = sb("pt_sb", [P, 2, 2, SW])
        zT = sb("zT", [P, 2, HALF, SEQ], F32R)
        mask = sb("mask", [P, SEQ])
        ident = sb("ident", [P, P])
        bn_parts = sb("bn_parts", [P, NT, 6])
        bn_mv = sb("bn_mv", [P, NT, 2])
        var_eps = sb("var_eps", [P, NT])
        rstd = sb("rstd", [P, NT])
        minus_half = sb("minus_half", [P, NT])
        euler = sb("euler", [P, NT * NE])
        neg_max = sb("neg_max", [P, 2, NT])
        row_sum = sb("row_sum", [P, 2, NT])
        row_inv = sb("row_inv", [P, 2, NT])
        b1_sb = sb("b1_sb", [P, NE])
        gate_raw = sb("gate_raw", [P, NC, 32])
        gates_w = sb("gates_w", [P, 2, NC, 32], F32R)
        pick = sb("pick", [P, NE], F32R)
        mv_moe = sb("mv_moe", [P, NT, 2])
        mean_moe = sb("mean_moe", [P, NT])
        shift_moe = sb("shift_moe", [P, NB * NT])
        rstd_moe = sb("rstd_moe", [P, NB * NT])
        var_moe = sb("var_moe", [P, NT])
        shift_now = sb("shift_now", [P, NT])
        rstd_now = sb("rstd_now", [P, NT])
        before = sb("before", [P, NE, NE])
        logit = sb("logit", [P, NT, NE])
        lmax = sb("lmax", [P, NT])
        gate = sb("gate", [P, NT, NE])
        gsum = sb("gsum", [P, NT])
        sel_pad = sb("sel_pad", [P, NT, 32])
        tok_w = sb("tok_w", [P, 2, NT])

        def w_part(i, part):
            return w_split[:, (2 * i + part) * WSZ:(2 * i + part + 1) * WSZ]

        wk, wq, wv = ([w_part(i, r).rearrange("p (c f) -> p c f", c=NC) for r in range(2)] for i in range(3))
        wo = [w_part(3, r).rearrange("p (g d) -> p g d", g=NG) for r in range(2)]

        w1s = [w_part(0, r).rearrange("p (e c h) -> p e c h", e=NE, c=NC) for r in range(2)]
        w2s = [w_part(1, r).rearrange("p (e d) -> p e d", e=NE) for r in range(2)]
        b2s = [w_part(2, 0)[:, r * D:(r + 1) * D] for r in range(2)]
        selT = [w_part(2, 0)[:, 2 * D + r * SEQ:2 * D + (r + 1) * SEQ] for r in range(2)]
        w1_raw = v_sb[:, :, 0:SEQ]
        spare = xn[:, :, :].rearrange("p t d -> p (t d)")
        rank_a = spare[:, 0:256].rearrange("p (t e f) -> p t e f", t=NT, e=NE)
        rank_b = spare[:, 256:512].rearrange("p (t e f) -> p t e f", t=NT, e=NE)
        rank = spare[:, 512:512 + NT * NE].rearrange("p (t e) -> p t e", t=NT)
        logitT = spare[0:32, 0:SEQ]
        b2_raw = spare[:, 768:768 + D]
        h_sb = [s_sb[:, r, 0:SEQ] for r in range(2)]
        h_sel = [pt_sb[:, 1, r, 0:SEQ] for r in range(2)]
        h_hi = [k_dup[:, 0, r, 0, :] for r in range(2)]
        h_lo = [k_dup[:, 0, r, 1, :] for r in range(2)]

        kq_bank = bank("kq_bank")
        aux_bank = bank("aux_bank")
        sc_bank = [bank(f"sc_bank{i}") for i in range(3)]
        pt_bank = [bank(f"pt_bank{i}") for i in range(2)]
        z_bank = bank("z_bank")
        up_bank = [kq_bank, pt_bank[0]]
        mask_bank = [pt_bank[1], z_bank]
        y_bank = sc_bank[0:2]
        route_bank = sc_bank[2]

        d_x0 = sem("d_x0")
        d_x1 = sem("d_x1")
        d_x = sem("d_x")
        d_w = [sem(f"d_attn_w{i}") for i in range(4)]
        d_small = sem("d_small")
        d_w1, d_w2, d_b2 = sem("d_w1"), sem("d_w2"), sem("d_b2")
        d_dup = sem("d_dup")
        d_out = sem("d_out")
        const_set = sem("const_set")
        w_hi, w_lo = sem("w_hi"), sem("w_lo")
        vo_lo = sem("vo_lo")
        ln_step = sem("ln_step")
        rstd_ready = sem("rstd_ready")
        pool_step = sem("pool_step")
        xn_ready = sem("xn_ready")
        aux_ready, aux_free = sem("aux_ready"), sem("aux_free")
        xn_hi = sem("xn_hi")
        xn_lo = sem("xn_lo")
        kq_ready = sem("kq_ready")
        kq_hi, kq_lo = sem("kq_hi"), sem("kq_lo")
        v_ready = sem("v_ready")
        sc_ready = sem("sc_ready")
        sc_masked = sem("sc_masked")
        exp_done = sem("exp_done")
        inv_done = sem("inv_done")
        p_ready = sem("p_ready")
        pt_ready = sem("pt_ready")
        pt_copied = sem("pt_copied")
        z_ready = sem("z_ready")
        z_hi, z_lo = sem("z_hi"), sem("z_lo")
        up_ready = sem("up_ready")
        h_ready = sem("h_ready")
        mask_ready = sem("mask_ready")
        h_sel_ready = sem("h_sel_ready")
        h_hi_ready, h_lo_ready = sem("h_hi_ready"), sem("h_lo_ready")
        y_ready = sem("y_ready")
        route_ready = sem("route_ready")
        logitT_ready = sem("logitT_ready")
        route_step = sem("route_step")
        route_exp = sem("route_exp")
        selT_ready = sem("selT_ready")
        ln_moe_step = sem("ln_moe_step")
        rstd_moe_ready = sem("rstd_moe_ready")
        mean_moe_ready, norm_step = sem("mean_moe_ready"), sem("norm_step")
        moe_pool_step = sem("moe_pool_step")
        gates_hi, gates_lo = sem("gates_hi"), sem("gates_lo")
        pick_ready = sem("pick_ready")
        moe_w_hi, moe_w_lo = sem("moe_w_hi"), sem("moe_w_lo")
        res_ready = sem("res_ready")
        zero_set = sem("zero_set")
        passed = sem("passed")

        V1_SLOTS = [(0, 1), (2, 0), (2, 1), (3, 0)]
        O1_SLOTS = [(1, 0), (1, 1)]
        XNT_SLOTS = [(3, 1), (4, 0)]
        V0_SLOTS = [(4, 1), (6, 0), (6, 1), (7, 0)]
        O0_SLOTS = [(5, 0), (5, 1)]
        STATS_SLOT, NORM_SLOT = (0, 0), (1, 0)
        MOE_STATS_SLOT = (4, 1)
        GATES_SLOT, W1_SLOT, W2_SLOT = (3, 1), (6, 0), (7, 0)
        LOGIT_SLOT, LOGIT_BACK_SLOT, SELECT_SLOT = (4, 1), (6, 0), (7, 1)

        def after(slot):
            p, ab = slot
            return (p, 1) if ab == 0 else (p + 1, 0)

        XNT_EXPERTS = [1, 2]
        LOGITS_AT, LOGIT_BACK_AT, SELT_AT = 3, 3, 7
        GATES_AT, SELECT_AT = 5, 6
        ROUTE = 12
        ROUTE_HEAD, ROUTE_GATES, ROUTE_COMPARE, ROUTE_SELECT = 2, 5, 6, 10

        def wait_z_used(eng, b, p):
            if p >= 0:
                wait(eng, aux_ready, b, AUX, aux_k(b, (K_O1 if p < HALF else K_O0)[1]) + 1)
            elif isinstance(b, int):
                wait(eng, aux_ready, b - 1, AUX, aux_k(b - 1, K_O0[1]) + 1)
            else:
                wait(eng, aux_ready, b, AUX, aux_k(b, K_O0[1]) + 1 - AUX)

        block = ctx.enter_context(nc.Block())

        def batches(eng, body):
            with eng.Fori(1, NB - 2, 2) as i:
                body(i, 1)
                body(i + 1, 0)

        def x_tiles(b, t, n):
            return x_sb[:, span(b * (NT * D) + t * D, n * D)]

        w_raw = [buf[:, :, 0:WSZ // 2] for buf in (pt_sb[:, 0], pt_sb[:, 1], s_sb, pt_sb[:, 1])]
        start_bank = end_bank = [aux_bank, z_bank]

        @block.sync
        def _(sp):
            sp.dma_start(x_tiles(0, 0, NT).rearrange("p (t d) -> p t d", t=NT),
                         x[0].rearrange("(t p) d -> p t d", p=P)).then_inc(d_x0, 16)
            weights = [w.rearrange("(c p) f -> p c f", p=P) for w in (wk_t, wq_t, wv_t)]
            for i in range(3):
                sp.dma_start(w_raw[i], weights[i]).then_inc(d_w[i], 16)
            sp.dma_start(x_tiles(1, 0, NT).rearrange("p (t d) -> p t d", t=NT),
                         x[1].rearrange("(t p) d -> p t d", p=P)).then_inc(d_x1, 16)
            sp.wait_ge(w_lo, 2)
            for c in range(2):
                sp.dma_start(w_raw[3][:, c, :].rearrange("p (g d) -> p g d", g=NG // 2),
                             wo_t[c * (F // 2):(c + 1) * (F // 2), :].rearrange("(g p) d -> p g d", p=P))\
                  .then_inc(d_w[3], 16)
            sp.dma_start(b1_sb[:, :], b1_t).then_inc(d_small, 16)
            sp.wait_ge(const_set, 7)
            sp.dma_start(gate_raw[:, :, 0:NE], gate_w.rearrange("(c p) e -> p c e", p=P)).then_inc(d_small, 16)

            def duplicate(b, per, k, buf):
                wait_alone(sp, kq_lo, b, 2 * per, 2 * k + 1, passed)
                wait(sp, d_dup, b, 32 * per, 32 * k)
                for head, (src, dst) in enumerate(((0, 64), (64, 0))):
                    sp.dma_start(k_dup[dst:dst + 64, buf, head, :, :].bitcast(F32),
                                 k_dup[src:src + 64, buf, head, :, :].bitcast(F32)).then_inc(d_dup, 16)

            def batch(b, first_pair=1, last_pair=NPAIR):
                for p in range(first_pair, last_pair + 1):
                    duplicate(b, NPAIR, p, p % 2)

            duplicate(0, 0, 0, 0)
            batch(0, last_pair=1)
            for b in range(2, NB):
                sp.dma_start(x_tiles(b, 0, NT).rearrange("p (t d) -> p t d", t=NT),
                             x[b].rearrange("(t p) d -> p t d", p=P)).then_inc(d_x, 16)
            batch(0, first_pair=2)
            batches(sp, lambda b, q: batch(b))
            batch(NB - 1, last_pair=NPAIR - 2)

            sp.wait_ge(z_ready, NPAIR * (NB - 1) + HALF)
            for a in range(NT):
                sp.dma_start(w1_raw[:, a, :].rearrange("p (e c h) -> p e c h", e=2, c=NC),
                             w1[2 * a:2 * a + 2].rearrange("e (c p) h -> p e c h", p=P)).then_inc(d_w1, 16)
            sp.wait_ge(zero_set, 1)
            for t in range(NT):
                sp.dma_start(b2_raw[32 * t:32 * t + NE, :], b2).then_inc(d_b2, 16)
            batch(NB - 1, NPAIR - 1, NPAIR - 1)
            sp.wait_ge(moe_w_lo, 1)
            for a in range(NT):
                sp.dma_start(w1_raw[:, a, :].rearrange("p (e d) -> p e d", e=2),
                             w2[2 * a:2 * a + 2].rearrange("e p d -> p e d")).then_inc(d_w2, 16)

            with sp.Fori(0, NB) as m:
                sp.wait_ge(res_ready, 2 * m + 2)
                sp.dma_start(out[span(m, 1)].rearrange("b (t p) d -> p (b t) d", p=P),
                             x_tiles(m, 0, NT).rearrange("p (t d) -> p t d", t=NT)).then_inc(d_out, 16)
            sp.wait_ge(d_out, 16 * NB)

        @block.gpsimd
        def _(pool):
            pool.memset(minus_half[:, :], -0.5).then_inc(const_set, 1)
            pool.memset(euler[:, :], EULER).then_inc(const_set, 1)
            pool.memset(ident[:, :], 0.0).then_inc(const_set, 1)
            pool.memset(mask[:, :], 0.0).then_inc(const_set, 1)
            pool.memset(before[:, :, :], 1.0).then_inc(const_set, 1)
            pool.memset(sel_pad[:, :, :], 0.0).then_inc(const_set, 1)
            pool.memset(gate_raw[:, :, :], 0.0).then_inc(const_set, 1)
            pool.wait_ge(const_set, 7)
            pool.affine_select(out=ident[:, :], in_=ident[:, :], compare_op=ALU.not_equal, fill=1.0,
                               base=0, pattern=[[-1, P]], channel_multiplier=1).then_inc(const_set, 1)
            pool.affine_select(out=mask[:, SEQ - P:SEQ], in_=mask[:, SEQ - P:SEQ], compare_op=ALU.is_ge,
                               fill=-NEG, base=0, pattern=[[-1, P]], channel_multiplier=1).then_inc(const_set, 1)
            pool.affine_select(out=before[:, :, :], in_=before[:, :, :], compare_op=ALU.is_ge, fill=0.0,
                               base=-1, pattern=[[1, NE], [-1, NE]], channel_multiplier=0).then_inc(const_set, 1)

            def rsqrt(c, k):
                wait_alone(pool, ln_step, c, 2, 2 * k + 2, passed)
                pool.tensor_scalar(var_eps[:, :], bn_mv[:, :, 1], EPS, None, ALU.add).then_inc(pool_step, 1)
                wait(pool, pool_step, c, 1, k + 1)
                pool.tensor_tensor(rstd[:, :], var_eps[:, :], minus_half[:, :], ALU.pow).then_inc(rstd_ready, 1)

            def rsqrt_moe(c, k):
                b = c + k
                wait_alone(pool, ln_moe_step, c, 2, 2 * k + 2, passed)
                pool.tensor_scalar(var_moe[:, :], mv_moe[:, :, 1], EPS, None, ALU.add)\
                    .then_inc(moe_pool_step, 1)
                wait(pool, moe_pool_step, c, 2, 2 * k + 1)
                pool.tensor_tensor(rstd_moe[:, span(b * NT, NT)], var_moe[:, :], minus_half[:, :], ALU.pow)\
                    .then_inc(moe_pool_step, 1)
                wait(pool, moe_pool_step, c, 2, 2 * k + 2)
                wait(pool, mean_moe_ready, c, 1, k + 1)
                pool.tensor_tensor(shift_moe[:, span(b * NT, NT)], mean_moe[:, :], rstd_moe[:, span(b * NT, NT)],
                                   ALU.mult).then_inc(rstd_moe_ready, 1)

            def route_exp_part(m, k):
                wait(pool, route_step, m, ROUTE, ROUTE * k + ROUTE_HEAD)
                pool.tensor_tensor(gate[:, :, :].rearrange("p t e -> p (t e)"), euler[:, :],
                                   logit[:, :, :].rearrange("p t e -> p (t e)"), ALU.pow).then_inc(route_exp, 1)

            def batch(b, q):
                rsqrt(b, 1)
                rsqrt_moe(b, -1)

            rsqrt(0, 0)
            for i in (2, 3):
                pool.wait_ge(w_hi, i + 1)
                pool.tensor_tensor(w_part(i, 1).rearrange("p (c f) -> p c f", c=2), w_raw[i],
                                   w_part(i, 0).rearrange("p (c f) -> p c f", c=2).bitcast(F32), ALU.subtract)\
                    .then_inc(vo_lo, 1)
            rsqrt(0, 1)
            batches(pool, batch)
            pool.wait_ge(aux_ready, AUX * (NB - 1) + aux_k(NB - 1, K_XNT[1]) + 1)
            pool.memset(b2_raw, 0.0).then_inc(zero_set, 1)
            rsqrt_moe(NB - 1, -1)

            def expert_weight_lo(count, src, hi, lo):
                pool.wait_ge(moe_w_hi, count)
                pool.tensor_tensor(lo, src, hi.bitcast(F32), ALU.subtract).then_inc(moe_w_lo, 1)

            expert_weight_lo(1, w1_raw, *(w_part(0, r).rearrange("p (a n) -> p a n", a=NT) for r in range(2)))
            route_exp_part(0, 0)
            expert_weight_lo(2, w1_raw, *(w_part(1, r).rearrange("p (a n) -> p a n", a=NT) for r in range(2)))
            expert_weight_lo(3, b2_raw, b2s[0], b2s[1])
            rsqrt_moe(NB, -1)
            route_exp_part(0, 1)
            batches(pool, lambda m, q: route_exp_part(m, 1))

        @block.scalar
        def _(act):
            def weight_hi(i, src, dst, landed, count, done):
                act.wait_ge(landed, count)
                act.activation(dst, src, ACT.Copy).then_inc(done, 1)

            def attention_weight_hi(i, count=16):
                weight_hi(i, w_raw[i], w_part(i, 0).rearrange("p (c f) -> p c f", c=2), d_w[i], count, w_hi)

            def xnt_hi(b, per, k, u, buf, bank=aux_bank):
                wait(act, aux_ready, b, per, k + 1)
                act.activation(xnT[:, buf, 0, u, :], bank[:, :], ACT.Copy).then_inc(xn_hi, 1)

            def v_unit(b, k, half, t):
                wait(act, aux_ready, b, AUX, aux_k(b, k) + 1)
                v_copy(half, t, aux_bank)

            def first_v_unit(t):
                act.wait_ge(aux_ready, NC + t + 1)
                v_copy(0, t, start_bank[t % 2])

            def v_copy(half, t, bank):
                act.activation(v_sb[:, t, half * SEQ:(half + 1) * SEQ], bank[:, :], ACT.Copy)\
                   .then_inc(aux_free, 1)

            def k_hi(b, p, buf):
                wait(act, kq_ready, b, 2 * NPAIR, 2 * p + 1)
                wait(act, d_dup, b, 32 * NPAIR, 32 * (p - 1))
                for head in range(2):
                    r = slice(64 * head, 64 * head + 64)
                    last = act.activation(k_dup[r, buf, head, 0, :], kq_bank[r, :], ACT.Copy)
                last.then_inc(kq_hi, 1)

            def q_hi(b, p, buf):
                wait(act, kq_ready, b, 2 * NPAIR, 2 * p + 2)
                for head in range(2):
                    r = slice(64 * head, 64 * head + 64)
                    last = act.activation(q_stk[r, buf, head, :], kq_bank[r, :], ACT.Copy)
                last.then_inc(kq_hi, 1)

            def exps(b, h, order):
                for t in order:
                    wait(act, sc_masked, b, 4 * NH, 4 * h + NT - t)
                    s = s_sb[:, h % 2, S_AT[t]:S_AT[t] + P * (t + 1)]
                    act.activation(s, s, ACT.Exp, bias=neg_max[:, h % 2, t:t + 1], scale=-1.0,
                                   accum_out=row_sum[:, h % 2, t:t + 1]).then_inc(exp_done, 1)

            def pt_copy(b, h, unit):
                n = 3 * h + unit
                wait(act, pt_ready, b, 3 * NH, n + 1)
                tiles, width = PT_UNITS[unit]
                at = PT_AT[tiles[0]]
                pair = h // 2
                if unit == 0:
                    wait(act, z_ready, b, NPAIR, pair - 1)
                act.activation(pt_sb[:, pair % 2, h % 2, at:at + width], pt_bank[n % 2][:, 0:width], ACT.Copy)\
                   .then_inc(pt_copied, 1)

            def z_part(b, p):
                wait(act, z_ready, b, NPAIR, p + 1)
                wait_z_used(act, b, p)
                act.activation(zT[:, 0, p % HALF, :], z_bank[:, :], ACT.Copy).then_inc(z_hi, 1)

            def normalise_moe(c, k, aux, ka, tiles=range(NT)):
                wait(act, norm_step, c, 1, k + 1)
                wait(act, aux_ready, *aux, ka)
                for t in tiles:
                    last = act.activation(xn[:, t, :], x_tiles(c + k, t, 1), ACT.Identity,
                                          bias=shift_now[:, t:t + 1], scale=rstd_now[:, t:t + 1])
                if NT - 1 in tiles:
                    last.then_inc(xn_ready, 1)

            def batch(b, q, first=False, last=False):
                for p in range(NPAIR):
                    for ab in range(2):
                        h = 2 * p + ab
                        slot = (p, ab)
                        if ab == 0 and not (first and p < 2):
                            z_part(b, p - 2)
                        if not (last and p == NPAIR - 1):
                            (k_hi if ab == 0 else q_hi)(b, p + 1, (p + 1) % 2)
                        for half, slots, ks in ((1, V1_SLOTS, K_V1), (0, V0_SLOTS, K_V0)):
                            for t in range(NT):
                                skip = last and half == 0
                                if slot == after(slots[t]) and not skip:
                                    v_unit(b, ks[t], half, t)
                        for u in range(NC):
                            if slot == after(XNT_SLOTS[u]):
                                xnt_hi(b, AUX, aux_k(b, K_XNT[u]), u, 1 - q)
                        if last and slot == after(LOGIT_SLOT):
                            logitT_copy(0, 0, aux_bank)
                        has_prev = not (first and h == 0)
                        if ab == 1:
                            exps(b, h, (3,))
                        if first and h == 3:
                            act.wait_ge(vo_lo, 2)
                        if has_prev:
                            pt_copy(b, h - 1, 0)
                        if ab == 0:
                            exps(b, h, (3,))
                        exps(b, h, (2,))
                        if has_prev:
                            pt_copy(b, h - 1, 1)
                        exps(b, h, (1, 0))
                        if has_prev:
                            pt_copy(b, h - 1, 2)
                        if first and h == 0:
                            for t in (2, 3):
                                first_v_unit(t)
                            attention_weight_hi(3, 32)
                        if last and slot == NORM_SLOT:
                            normalise_moe(0, 0, (b, AUX), aux_k(0, K_XNT[1]) + 1 - AUX)
                        if last:
                            prepare_experts(slot)

            def prepare_experts(slot):
                if slot == GATES_SLOT:
                    weight_hi(2, gate_raw[:, :, :], gates_w[:, 0], d_small, 32, gates_hi)
                    for t in range(NT):
                        r = slice(32 * t, 32 * t + 32)
                        last = act.activation(pick[r, :], ident[r, 32 * t:32 * t + NE], ACT.Copy)
                    last.then_inc(pick_ready, 1)
                if slot == W1_SLOT:
                    weight_hi(0, w1_raw, w_part(0, 0).rearrange("p (a n) -> p a n", a=NT), d_w1, 16 * NT, moe_w_hi)
                    for buf in range(2):
                        act.activation(selT[buf].rearrange("p (a n) -> p a n", a=2),
                                       mask[:, 0:SEQ // 2].unsqueeze(1).broadcast_to([P, 2, SEQ // 2]), ACT.Copy)
                if slot == W2_SLOT:
                    weight_hi(1, w1_raw, w_part(1, 0).rearrange("p (a n) -> p a n", a=NT), d_w2, 16 * NT, moe_w_hi)
                    weight_hi(2, b2_raw, b2s[0], d_b2, 16 * NT, moe_w_hi)

            def logitT_copy(m, k, bank):
                wait(act, route_ready, m, 3, 3 * k + 1)
                act.activation(logitT, bank[0:32, :], ACT.Copy).then_inc(logitT_ready, 1)

            attention_weight_hi(0)
            for u in range(NC):
                xnt_hi(0, 0, u, u, 0, start_bank[u])
            attention_weight_hi(1)
            attention_weight_hi(2)
            k_hi(0, 0, 0)
            q_hi(0, 0, 0)
            for t in range(2):
                first_v_unit(t)
            batch(0, 0, first=True)
            batches(act, lambda b, q: batch(b, q))
            batch(NB - 1, 1, last=True)
            z_part(NB, -2)
            for unit in range(3):
                pt_copy(NB, -1, unit)

            def selT_copy(m, k, q):
                wait(act, route_ready, m, 3, 3 * k + 3)
                for t in range(NT):
                    act.activation(selT[q][32 * t:32 * t + 32, t * P:(t + 1) * P],
                                   route_bank[32 * t:32 * t + 32, 0:P], ACT.Copy).then_inc(selT_ready, 1)

            def experts(m, q, last=False):
                for e in range(NE):
                    wait(act, up_ready, m, NE, e + 1)
                    wait(act, h_sel_ready, m, NE, e - 1)
                    act.activation(h_sb[e % 2], up_bank[e % 2][:, :], ACT.Gelu, bias=b1_sb[:, e:e + 1])\
                       .then_inc(h_ready, 1)
                    if not last and e == 0:
                        normalise_moe(m, 1, (m, 2), aux_moe, (0, 1))
                    wait(act, h_sel_ready, m, NE, e + 1)
                    wait(act, y_ready, m, NE, e - 1)
                    act.activation(h_hi[e % 2], h_sel[e % 2], ACT.Copy).then_inc(h_hi_ready, 1)
                    if not last and e == 0:
                        normalise_moe(m, 1, (m, 2), aux_moe, (2, 3))
                    if not last and e in XNT_EXPERTS:
                        u = XNT_EXPERTS.index(e)
                        xnt_hi(m, 2, aux_moe + u, u, 1 - q)
                    if not last and e == LOGITS_AT:
                        logitT_copy(m, 1, route_bank)
                    if not last and e == SELT_AT:
                        selT_copy(m, 1, 1 - q)

            selT_copy(0, 0, 0)
            z_part(NB, -1)
            act.wait_ge(moe_w_lo, 3)
            experts(0, 0)
            batches(act, lambda m, q: experts(m, q))
            experts(NB - 1, 1, last=True)

        @block.vector
        def _(dve):
            def weight_lo(src, hi, dst, ready, count, done):
                dve.wait_ge(ready, count)
                dve.tensor_tensor(dst, src, hi.bitcast(F32), ALU.subtract).then_inc(done, 1)

            def stats(c, k, b):
                for t in range(NT):
                    last = dve.bn_stats(bn_parts[:, t, :], x_tiles(b, t, 1))
                last.then_inc(ln_step, 1)
                wait_alone(dve, ln_step, c, 2, 2 * k + 1, passed)
                for t in range(NT):
                    last = dve.bn_aggr(bn_mv[:, t, :], bn_parts[:, t, :])
                last.then_inc(ln_step, 1)

            def stats_moe(c, k):
                b = c + k
                if isinstance(b, int):
                    dve.wait_ge(rstd_moe_ready, b)
                for t in range(NT):
                    last = dve.bn_stats(bn_parts[:, t, :], x_tiles(b, t, 1))
                last.then_inc(ln_moe_step, 1)
                wait_alone(dve, ln_moe_step, c, 2, 2 * k + 1, passed)
                for t in range(NT):
                    last = dve.bn_aggr(mv_moe[:, t, :], bn_parts[:, t, :])
                last.then_inc(ln_moe_step, 1)
                wait(dve, ln_moe_step, c, 2, 2 * k + 2)
                dve.tensor_scalar(mean_moe[:, :], mv_moe[:, :, 0], -1.0, None, ALU.mult)\
                   .then_inc(mean_moe_ready, 1)

            def norm_factors(c, k):
                b = c + k
                wait(dve, rstd_moe_ready, c, 1, k + 1)
                wait(dve, xn_ready, c, 1, NB + k)
                dve.tensor_scalar(shift_now[:, :], shift_moe[:, span(b * NT, NT)], 1.0, None, ALU.mult)
                dve.tensor_scalar(rstd_now[:, :], rstd_moe[:, span(b * NT, NT)], 1.0, None, ALU.mult)\
                   .then_inc(norm_step, 1)

            def normalise(c, k, b, aux, ka):
                wait(dve, rstd_ready, c, 1, k + 1)
                wait(dve, aux_ready, *aux, ka)
                for t in range(NT):
                    last = dve.tensor_scalar(xn[:, t, :], x_tiles(b, t, 1), bn_mv[:, t, 0:1],
                                             rstd[:, t:t + 1], ALU.subtract, ALU.mult)
                last.then_inc(xn_ready, 1)

            def xnt_lo(c, k, u, buf, bank=aux_bank):
                wait(dve, xn_hi, c, 2, 2 * k + u + 1)
                dve.tensor_tensor(xnT[:, buf, 1, u, :], bank[:, :], xnT[:, buf, 0, u, :].bitcast(F32),
                                  ALU.subtract).then_inc(aux_free, 1)

            def k_lo(b, p, buf):
                wait(dve, kq_hi, b, 2 * NPAIR, 2 * p + 1)
                for head in range(2):
                    r = slice(64 * head, 64 * head + 64)
                    last = dve.tensor_tensor(k_dup[r, buf, head, 1, :], kq_bank[r, :],
                                             k_dup[r, buf, head, 0, :].bitcast(F32), ALU.subtract)
                last.then_inc(kq_lo, 1)

            def q_lo(b, p, buf):
                wait(dve, kq_hi, b, 2 * NPAIR, 2 * p + 2)
                for head in range(2):
                    r = slice(64 * head, 64 * head + 64)
                    o = slice(64 - 64 * head, 128 - 64 * head)
                    last = dve.tensor_tensor(q_stk[o, buf, head, :], kq_bank[r, :],
                                             q_stk[r, buf, head, :].bitcast(F32), ALU.subtract)
                last.then_inc(kq_lo, 1)

            def mask_and_max(b, h):
                wait(dve, pt_ready, b, 3 * NH, 3 * (h - 1))
                for unit, (tiles, cols) in enumerate(SC_UNITS):
                    wait_alone(dve, sc_ready, b, 3 * NH, 3 * h + unit + 1, passed)
                    for t, at in zip(tiles, cols):
                        n = P * (t + 1)
                        dve.tensor_tensor_reduce(
                            out=s_sb[:, h % 2, S_AT[t]:S_AT[t] + n], in0=sc_bank[unit][:, at:at + n],
                            in1=mask[:, SEQ - n:SEQ], scale=-SCALE, scalar=FLT_MAX, op0=ALU.add, op1=ALU.min,
                            accum_out=neg_max[:, h % 2, t:t + 1]).then_inc(sc_masked, 1)

            def divide(b, h):
                for i, (lo_t, hi_t) in enumerate(((2, 4), (0, 2))):
                    wait(dve, exp_done, b, 4 * NH, 4 * h + 2 * i + 2)
                    dve.reciprocal(row_inv[:, h % 2, lo_t:hi_t], row_sum[:, h % 2, lo_t:hi_t]).then_inc(inv_done, 1)
                    wait(dve, inv_done, b, 2 * NH, 2 * h + i + 1)
                    for t in (hi_t - 1, lo_t):
                        s = s_sb[:, h % 2, S_AT[t]:S_AT[t] + P * (t + 1)]
                        last = dve.tensor_scalar(s, s, row_inv[:, h % 2, t:t + 1], None, ALU.mult)
                    last.then_inc(p_ready, 1)

            def z_part(b, p):
                wait(dve, z_hi, b, NPAIR, p + 1)
                dve.tensor_tensor(zT[:, 1, p % HALF, :], z_bank[:, :], zT[:, 0, p % HALF, :].bitcast(F32),
                                  ALU.subtract).then_inc(z_lo, 1)

            def add_output(b, k, b_x, u):
                wait(dve, aux_ready, b, AUX, aux_k(b, k) + 1)
                dve.tensor_tensor(x_tiles(b_x, 2 * u, 2), x_tiles(b_x, 2 * u, 2), aux_bank[:, :], ALU.add)\
                   .then_inc(aux_free, 1)

            def linker(m, k, first):
                step = [first]

                def link(ins):
                    step[0] += 1
                    ins.then_inc(route_step, 1)
                    wait(dve, route_step, m, ROUTE, ROUTE * k + step[0])

                return link, step

            def route_head(m, k, bank):
                link, step = linker(m, k, 0)
                lg = bank[:, 0:P].rearrange("p (t e) -> p t e", t=NT)[:, :, 0:NE]
                tile_bc = [P, NT, NE]
                wait(dve, route_ready, m, 3, 3 * k + 2)
                link(dve.tensor_reduce(lmax[:, :], lg, AX.X, ALU.max))
                ins = dve.tensor_tensor(logit[:, :, :], lg, lmax[:, :].unsqueeze(2).broadcast_to(tile_bc), ALU.subtract)
                link(ins)
                assert step[0] == ROUTE_HEAD

            def gates(m, k):
                link, step = linker(m, k, ROUTE_HEAD)
                tile_bc = [P, NT, NE]
                wait(dve, route_exp, m, 1, k + 1)
                link(dve.tensor_reduce(gsum[:, :], gate[:, :, :], AX.X, ALU.add))
                link(dve.reciprocal(gsum[:, :], gsum[:, :]))
                link(dve.tensor_tensor(gate[:, :, :], gate[:, :, :], gsum[:, :].unsqueeze(2).broadcast_to(tile_bc),
                                       ALU.mult))
                assert step[0] == ROUTE_GATES

            def compare(m, k):
                link, step = linker(m, k, ROUTE_GATES)
                other = gate[:, :, :].unsqueeze(2).broadcast_to([P, NT, NE, NE])
                own = gate[:, :, :].unsqueeze(3).broadcast_to([P, NT, NE, NE])
                dve.tensor_tensor(rank_a, other, own, ALU.is_gt)
                link(dve.tensor_tensor(rank_b, other, own, ALU.is_equal))
                assert step[0] == ROUTE_COMPARE

            def select(m, k):
                link, step = linker(m, k, ROUTE_COMPARE)
                link(dve.tensor_tensor(rank_b, rank_b, before[:, :, :].unsqueeze(1).broadcast_to([P, NT, NE, NE]),
                                       ALU.mult))
                link(dve.tensor_tensor(rank_a, rank_a, rank_b, ALU.add))
                link(dve.tensor_reduce(rank, rank_a, AX.X, ALU.add))
                wait(dve, route_ready, m, 3, 3 * k)
                link(dve.tensor_scalar(sel_pad[:, :, 0:NE], rank, 1.5, None, ALU.is_lt))
                assert step[0] == ROUTE_SELECT

            def token_weights(m, k, q):
                link, step = linker(m, k, ROUTE_SELECT)
                link(dve.tensor_tensor(gate[:, :, :], gate[:, :, :], sel_pad[:, :, 0:NE], ALU.mult))
                link(dve.tensor_reduce(tok_w[:, q, :], gate[:, :, :], AX.X, ALU.add))
                assert step[0] == ROUTE

            def batch(b, q, first=False, last=False):
                for p in range(NPAIR):
                    for ab in range(2):
                        h = 2 * p + ab
                        slot = (p, ab)
                        for slots, ks, b_x in ((O1_SLOTS, K_O1, b - 1), (O0_SLOTS, K_O0, b)):
                            for u in range(2):
                                if slot == after(slots[u]) and not (first and slots == O1_SLOTS):
                                    add_output(b, ks[u], b_x, u)
                        if ab == 0 and not (first and p < 2):
                            z_part(b, p - 2)
                        mask_and_max(b, h)
                        for u in range(NC):
                            if slot == after(XNT_SLOTS[u]):
                                xnt_lo(b, 1, u, 1 - q)
                        if not (last and p == NPAIR - 1):
                            (k_lo if ab == 0 else q_lo)(b, p + 1, (p + 1) % 2)
                        divide(b, h)
                        if slot == STATS_SLOT and not last:
                            if first:
                                dve.wait_ge(d_x1, 16)
                            stats(b, 1, b + 1)
                        if slot == NORM_SLOT and not last:
                            normalise(b, 1, b + 1, (b, AUX), aux_k(0, K_XNT[1]) + 1 - AUX)
                        if slot == NORM_SLOT and last:
                            norm_factors(0, 0)
                        if slot == MOE_STATS_SLOT and first:
                            dve.wait_ge(d_x, 16 * (NB - 2))
                        if slot == MOE_STATS_SLOT and not first:
                            stats_moe(b, -1)
                        if last:
                            prepare_experts(slot)

            def prepare_experts(slot):
                if slot == GATES_SLOT:
                    weight_lo(gate_raw[:, :, :], gates_w[:, 0], gates_w[:, 1], gates_hi, 1, gates_lo)
                if slot == after(LOGIT_BACK_SLOT):
                    route_head(0, 0, aux_bank)
                if slot == SELECT_SLOT:
                    gates(0, 0)
                    compare(0, 0)
                    select(0, 0)
                    token_weights(0, 0, 0)

            dve.wait_ge(d_x0, 16)
            stats(0, 0, 0)
            normalise(0, 0, 0, (0, 0), 0)
            for u in range(NC):
                xnt_lo(0, 0, u, 0, start_bank[u])
            for i in range(2):
                weight_lo(w_raw[i], w_part(i, 0).rearrange("p (c f) -> p c f", c=2),
                          w_part(i, 1).rearrange("p (c f) -> p c f", c=2), w_hi, i + 1, w_lo)
            k_lo(0, 0, 0)
            q_lo(0, 0, 0)
            dve.wait_ge(vo_lo, 1)
            dve.wait_ge(const_set, 10)
            batch(0, 0, first=True)
            batches(dve, lambda b, q: batch(b, q))
            batch(NB - 1, 1, last=True)
            z_part(NB, -2)
            z_part(NB, -1)

            def add_last_outputs():
                for u in range(2):
                    dve.wait_ge(aux_ready, aux_o1_last + u + 1)
                    dve.tensor_tensor(x_tiles(NB - 1, 2 * u, 2), x_tiles(NB - 1, 2 * u, 2), end_bank[u][:, :],
                                      ALU.add).then_inc(aux_free, 1)

            def result(m, q, k=0, tiles=range(NT)):
                wait(dve, y_ready, m, NE, NE * (k + 1))
                for t in tiles:
                    last = dve.scalar_tensor_tensor(
                        x_tiles(m + k, t, 1), y_bank[t // 2][:, (t % 2) * D:(t % 2) * D + D],
                        tok_w[:, q, t:t + 1], x_tiles(m + k, t, 1), ALU.mult, ALU.add)
                    if t % 2 == 1:
                        last.then_inc(res_ready, 1)

            def experts(m, q, first=False, last=False):
                if not last:
                    norm_factors(m, 1)
                for e in range(NE):
                    if not last and e == XNT_EXPERTS[0] + 1:
                        xnt_lo(m, NB + 1, 0, 1 - q)
                    if not last and e == XNT_EXPERTS[1] + 1:
                        xnt_lo(m, NB + 1, 1, 1 - q)
                    if not last and e == LOGIT_BACK_AT + 1:
                        route_head(m, 1, route_bank)
                    wait(dve, h_ready, m, NE, e + 1)
                    wait(dve, mask_ready, m, NE, e + 1)
                    wait(dve, h_hi_ready, m, NE, e - 1)
                    dve.tensor_tensor(h_sel[e % 2], h_sb[e % 2], mask_bank[e % 2][:, :], ALU.mult)\
                       .then_inc(h_sel_ready, 1)
                    if not first and e == 0:
                        result(m, 1 - q, -1, (0, 1))
                    if first and e == 0:
                        add_last_outputs()
                    if first and e == 1:
                        dve.wait_ge(aux_free, aux_moe)
                        stats_moe(NB, -1)
                    if not last and e == SELECT_AT:
                        compare(m, 1)
                    if not last and e == SELECT_AT + 1:
                        token_weights(m, 1, 1 - q)
                    wait(dve, h_hi_ready, m, NE, e + 1)
                    dve.tensor_tensor(h_lo[e % 2], h_sel[e % 2], h_hi[e % 2].bitcast(F32), ALU.subtract)\
                       .then_inc(h_lo_ready, 1)
                    if not first and e == 0:
                        result(m, 1 - q, -1, (2, 3))
                    if not last and e == GATES_AT:
                        gates(m, 1)
                    if not last and e == SELECT_AT:
                        select(m, 1)

            experts(0, 0, first=True)
            batches(dve, lambda m, q: experts(m, q))
            experts(NB - 1, 1, last=True)
            result(NB - 1, 1)

        @block.tensor
        def _(pe):
            def split_product(out_ap, pairs):
                terms = [(s[i], v[j]) for s, v in pairs for i, j in ((0, 0), (0, 1), (1, 0))]
                for n, (s, v) in enumerate(terms):
                    last = pe.matmul(out_ap, s, v, start=(n == 0), stop=(n == len(terms) - 1))
                return last

            def k_or_q(b, p, w, unit, buf, cols):
                wait(pe, kq_lo, b, 2 * NPAIR, 2 * p + unit)
                split_product(kq_bank[:, :],
                              [([w[r][:, c, cols * P:(cols + 1) * P] for r in range(2)],
                                [xnT[:, buf, r, c, :] for r in range(2)]) for c in range(NC)]).then_inc(kq_ready, 1)

            def v_unit(b, k, half, t, buf):
                wait_aux(b, k)
                v_product(half, t, buf, aux_bank)

            def v_product(half, t, buf, bank):
                split_product(bank[:, :],
                              [([xnT[:, buf, r, c, t * P:(t + 1) * P] for r in range(2)],
                                [wv[r][:, c, half * SEQ:(half + 1) * SEQ] for r in range(2)]) for c in range(NC)])\
                    .then_inc(aux_ready, 1)

            def wait_aux(b, k):
                wait(pe, aux_free, b, AUX, aux_k(b, k))

            def xnt_unit(u, bank=aux_bank):
                for t in range(NT):
                    last = pe.transpose(bank[:, t * P:(t + 1) * P], xn[:, t, u * P:(u + 1) * P], ident[:, :])
                last.then_inc(aux_ready, 1)

            def output_unit(u, half, bank=aux_bank):
                for t in (2 * u, 2 * u + 1):
                    last = split_product(bank[:, (t % 2) * D:(t % 2) * D + D],
                                         [([zT[:, r, g, t * P:(t + 1) * P] for r in range(2)],
                                           [wo[r][:, half * HALF + g, :] for r in range(2)]) for g in range(HALF)])
                last.then_inc(aux_ready, 1)

            def scores(b, h):
                p, head = h // 2, h % 2
                if head == 0:
                    wait(pe, kq_lo, b, 2 * NPAIR, 2 * p + 2)
                    wait(pe, d_dup, b, 32 * NPAIR, 32 * (p + 1))
                for unit, (tiles, cols) in enumerate(SC_UNITS):
                    wait(pe, sc_masked, b, 4 * NH, 4 * (h - 1) + (1, 2, 4)[unit])
                    for t, at in zip(tiles, cols):
                        n = P * (t + 1)
                        for part in range(2):
                            last = pe.matmul(sc_bank[unit][:, at:at + n],
                                             q_stk[:, p % 2, head, t * P:(t + 1) * P],
                                             k_dup[:, p % 2, head, part, 0:n], start=(part == 0), stop=(part == 1))
                    last.then_inc(sc_ready, 1)

            def transposes(b, h, units):
                wait(pe, p_ready, b, 2 * NH, 2 * (h + 1))
                for unit in units:
                    n = 3 * h + unit
                    wait(pe, pt_copied, b, 3 * NH, n - 1)
                    at = 0
                    for j in PT_UNITS[unit][0]:
                        for t in range(j, NT):
                            col = S_AT[t] + j * P
                            last = pe.transpose(pt_bank[n % 2][:, at:at + P], s_sb[:, h % 2, col:col + P], ident[:, :])
                            at += P
                    last.then_inc(pt_ready, 1)

            def head_outputs(b, p, keys):
                wait(pe, pt_copied, b, 3 * NH, 6 * p + 4 if keys[0] == 0 else 6 * p + 6)
                if keys[0] == 0:
                    wait(pe, z_lo, b, NPAIR, p)
                    if p == 0:
                        wait(pe, aux_free, b, AUX, 6 if isinstance(b, int) and b == 0 else 4)
                    if p == HALF:
                        wait_aux(b, K_V1[3] + 1)
                for j in keys:
                    for head in range(2):
                        n = SEQ - j * P
                        f = (2 * p + head) % NH * DH
                        last = pe.matmul(z_bank[64 * head:64 * head + 64, j * P:SEQ], v_sb[:, j, f:f + DH],
                                         pt_sb[:, p % 2, head, PT_AT[j]:PT_AT[j] + n],
                                         start=(j == 0), stop=(j == NT - 1))
                if keys[-1] == NT - 1:
                    last.then_inc(z_ready, 1)

            def logitT_unit(m, k, buf, bank):
                split_product(bank[0:32, :], [([gates_w[:, r, c, :] for r in range(2)],
                                               [xnT[:, buf, r, c, :] for r in range(2)])
                                              for c in range(NC)]).then_inc(route_ready, 1)

            def logit_unit(m, k, bank):
                wait_alone(pe, logitT_ready, m, 1, k + 1, passed)
                for t in range(NT):
                    last = pe.transpose(bank[:, 32 * t:32 * t + 32], logitT[:, t * P:(t + 1) * P], ident[0:32, 0:32])
                last.then_inc(route_ready, 1)

            def selT_unit(m, k):
                wait(pe, route_step, m, ROUTE, ROUTE * k + ROUTE_SELECT)
                pe.transpose(route_bank[:, 0:P], sel_pad[:, :, :].rearrange("p t e -> p (t e)"), ident[:, :])\
                  .then_inc(route_ready, 1)

            def up(m, e, q):
                wait(pe, h_ready, m, NE, e - 1)
                split_product(up_bank[e % 2][:, :],
                              [([w1s[r][:, e, c, :] for r in range(2)],
                                [xnT[:, q, r, c, :] for r in range(2)]) for c in range(NC)]).then_inc(up_ready, 1)

            def mask_unit(m, e, q):
                if e == 0:
                    wait(pe, selT_ready, m, NT, NT)
                wait(pe, h_sel_ready, m, NE, e - 1)
                pe.matmul(mask_bank[e % 2][:, :], pick[:, e:e + 1].broadcast_to([P, P]), selT[q],
                          start=True, stop=True).then_inc(mask_ready, 1)

            def down(m, e, q):
                wait(pe, h_lo_ready, m, NE, e + 1)
                for t in range(NT):
                    y = y_bank[t // 2][:, (t % 2) * D:(t % 2) * D + D]
                    if e == 0:
                        if t % 2 == 0:
                            wait(pe, res_ready, m, 2, t // 2 - 1)
                        for r in range(2):
                            pe.matmul(y, selT[q][:, t * P:(t + 1) * P], b2s[r],
                                      start=(t % 2 == 0 and r == 0), stop=False)
                    h = [h_hi[e % 2][:, t * P:(t + 1) * P], h_lo[e % 2][:, t * P:(t + 1) * P]]
                    for i, j in ((0, 0), (0, 1), (1, 0)):
                        last = pe.matmul(y, h[i], w2s[j][:, e % NE, :], start=False,
                                         stop=(e % NE == NE - 1 and t % 2 == 1 and i == 1))
                last.then_inc(y_ready, 1)

            def experts(m, q, first=False, last=False):
                for e in range(NE):
                    if not (first and e < 2):
                        up(m, e, q)
                    if first and e == 1:
                        pe.wait_ge(aux_free, aux_moe)
                    if not (first and e == 0):
                        mask_unit(m, e, q)
                    if not last and e == LOGITS_AT:
                        wait(pe, aux_free, m, 2, aux_moe + 2)
                        logitT_unit(m, 1, 1 - q, route_bank)
                    if not (first and e == 0):
                        down(m, e - 1, q if e > 0 else 1 - q)
                    if not last and e == SELT_AT:
                        selT_unit(m, 1)
                    if not last and e == LOGIT_BACK_AT:
                        logit_unit(m, 1, route_bank)
                    if not last and e in XNT_EXPERTS:
                        u = XNT_EXPERTS.index(e)
                        wait(pe, xn_ready, m, 1, NB + 2)
                        wait(pe, aux_free, m, 2, aux_moe + u)
                        xnt_unit(u)

            def batch(b, q, first=False, last=False):
                for p in range(NPAIR):
                    for ab in range(2):
                        h = 2 * p + ab
                        slot = (p, ab)
                        scores(b, h)
                        if first and h == 0:
                            for t in (2, 3):
                                pe.wait_ge(aux_free, t + 1)
                                v_product(0, t, 0, start_bank[t % 2])
                        if not (first and h == 0):
                            transposes(b, h - 1, (0, 1))
                        if ab == 1 and not (first and p == 0):
                            head_outputs(b, p - 1, (1, 2, 3))
                        for half, slots, ks in ((1, V1_SLOTS, K_V1), (0, V0_SLOTS, K_V0)):
                            for t in range(NT):
                                skip = last and half == 0
                                if slot == slots[t] and not skip:
                                    v_unit(b, ks[t], half, t, 1 - q if half == 0 else q)
                        if not (first and h == 0):
                            transposes(b, h - 1, (2,))
                        if ab == 0 and not (first and p == 0):
                            head_outputs(b, p - 1, (0,))
                        for u in range(NC):
                            if slot == XNT_SLOTS[u]:
                                wait(pe, xn_ready, b, 1, 2)
                                wait_aux(b, K_XNT[u])
                                xnt_unit(u)
                        if last and slot == LOGIT_SLOT:
                            pe.wait_ge(gates_lo, 1)
                            wait_aux(b, K_V0[0])
                            logitT_unit(0, 0, 0, aux_bank)
                        if last and slot == O0_SLOTS[0]:
                            pe.wait_ge(logitT_ready, 1)
                        for half, slots, ks in ((1, O1_SLOTS, K_O1), (0, O0_SLOTS, K_O0)):
                            for u in range(2):
                                if slot == slots[u] and not (first and half == 1):
                                    if first and u == 0:
                                        pe.wait_ge(vo_lo, 2)
                                    wait(pe, z_lo, b, NPAIR, HALF * (1 - half))
                                    wait_aux(b, ks[u])
                                    output_unit(u, half)
                        if last and slot == LOGIT_BACK_SLOT:
                            pe.wait_ge(aux_free, aux_o1_last)
                            logit_unit(0, 0, aux_bank)
                        pair = p + 1 + ab
                        if not (last and pair >= NPAIR):
                            k_or_q(b, pair, (wq, wk)[ab], 1 - ab, q if pair < NPAIR else 1 - q, pair % NPAIR)

            pe.wait_ge(const_set, 8)
            pe.wait_ge(xn_ready, 1)
            for u in range(NC):
                xnt_unit(u, start_bank[u])
            pe.wait_ge(aux_free, NC)
            pe.wait_ge(w_lo, 1)
            k_or_q(0, 0, wk, 0, 0, 0)
            pe.wait_ge(w_lo, 2)
            k_or_q(0, 0, wq, 1, 0, 0)
            pe.wait_ge(vo_lo, 1)
            for t in range(2):
                v_product(0, t, 0, start_bank[t])
            k_or_q(0, 1, wk, 0, 0, 1)
            batch(0, 0, first=True)
            batches(pe, lambda b, q: batch(b, q))
            batch(NB - 1, 1, last=True)
            pe.wait_ge(moe_w_lo, 1)
            up(0, 0, 0)
            transposes(NB, -1, (0, 1, 2))
            head_outputs(NB, -1, (0,))
            pe.wait_ge(sc_masked, 4 * NH * NB)
            selT_unit(0, 0)
            head_outputs(NB, -1, (1, 2, 3))
            up(0, 1, 0)
            pe.wait_ge(pick_ready, 1)
            mask_unit(0, 0, 0)
            pe.wait_ge(z_lo, NPAIR * NB)
            for u in range(2):
                output_unit(u, 1, end_bank[u])
            pe.wait_ge(moe_w_lo, 3)
            experts(0, 0, first=True)
            batches(pe, lambda m, q: experts(m, q))
            experts(NB - 1, 1, last=True)
            down(NB, -1, 1)


def kernel(L0_attn_x, L0_attn_W_K, L0_attn_W_Q, L0_attn_W_V, L0_attn_W_O, L0_ffn_gate_w,
           L0_ffn_w1, L0_ffn_b1, L0_ffn_w2, L0_ffn_b2):
    import numpy as np
    import concourse.bacc as bacc
    from concourse.bass_utils import run_bass_kernel_spmd

    def rows(w):
        w = np.asarray(w)
        return np.ascontiguousarray(w.reshape(-1, w.shape[-1]).T)

    arrays = {
        "x": np.ascontiguousarray(L0_attn_x),
        "wq_t": rows(L0_attn_W_Q),
        "wk_t": rows(L0_attn_W_K),
        "wv_t": rows(L0_attn_W_V),
        "wo_t": np.ascontiguousarray(np.asarray(L0_attn_W_O).T),
        "gate_w": np.ascontiguousarray(L0_ffn_gate_w),
        "w1": np.ascontiguousarray(L0_ffn_w1),
        "b1_t": np.ascontiguousarray(np.asarray(L0_ffn_b1).T),
        "w2": np.ascontiguousarray(L0_ffn_w2),
        "b2": np.ascontiguousarray(L0_ffn_b2),
    }
    nc = bacc.Bacc("TRN2", target_bir_lowering=False, num_devices=1)
    args = {k: nc.dram_tensor(k, a.shape, mybir.dt.from_np(a.dtype), kind="ExternalInput").ap()
            for k, a in arrays.items()}
    y = nc.dram_tensor("y", arrays["x"].shape, F32, kind="ExternalOutput").ap()
    build_layer(nc, out=y, **args)
    r = run_bass_kernel_spmd(nc, [arrays], core_ids=[0])
    return r.results[0]["y"]
```
